# Optimizing a Trainium2 kernel written in Bass

```python
import numpy as np
import jax
import jax.numpy as jnp

def _softmax(x, axis=-1):
    return jax.nn.softmax(x, axis=axis)

def _gelu(x):
    return jax.nn.gelu(x, approximate=True)

def _silu(x):
    return jax.nn.silu(x)

def _sigmoid(x):
    return jax.nn.sigmoid(x)

def _layernorm(x, axis=-1, eps=1e-05):
    m = jnp.mean(x, axis=axis, keepdims=True)
    v = jnp.var(x, axis=axis, keepdims=True)
    return (x - m) / jnp.sqrt(v + eps)

def _scatter_add(tgt, idx, src, axis=0):
    return tgt.at[idx].add(src)

def _segment_sum(src, seg, n):
    return jax.ops.segment_sum(src, seg, n)
kernel_name = 'mk_seq_postln_d1_jaxref_r4_96a1fb'

def setup_inputs(seed: int=0):
    np.random.seed(seed)
    _w = jnp.asarray

    def _L0_attn_setup():
        import jax, jax.numpy as jnp
        import numpy as np
        B, T, D, H = (4, 512, 256, 16)
        HD = D // H
        NEG = -np.finfo(np.float32).max
        key = jax.random.key(seed)
        ks = jax.random.split(key, 9)
        s = 1.0 / np.sqrt(D)
        return {'x': jax.random.normal(ks[0], (B, T, D), jnp.float32), 'wq': jax.random.normal(ks[1], (D, D), jnp.float32) * s, 'bq': jax.random.normal(ks[2], (D,), jnp.float32) * 0.02, 'wk': jax.random.normal(ks[3], (D, D), jnp.float32) * s, 'bk': jax.random.normal(ks[4], (D,), jnp.float32) * 0.02, 'wv': jax.random.normal(ks[5], (D, D), jnp.float32) * s, 'bv': jax.random.normal(ks[6], (D,), jnp.float32) * 0.02, 'wo': jax.random.normal(ks[7], (D, D), jnp.float32) * s, 'bo': jax.random.normal(ks[8], (D,), jnp.float32) * 0.02}
    _L0_attn_in = _L0_attn_setup()

    def _L0_ffn_setup():
        import jax, jax.numpy as jnp
        import numpy as np
        D_MODEL = 256
        D_FF = 1024
        NUM_EXPERTS = 8
        B, N = (16, 256)
        key = jax.random.key(seed)
        ks = jax.random.split(key, 7)
        s_in = 1.0 / np.sqrt(D_MODEL)
        s_ff = 1.0 / np.sqrt(D_FF)
        return {'x': jax.random.normal(ks[0], (B, N, D_MODEL), dtype=jnp.float32), 'Wr': jax.random.uniform(ks[1], (D_MODEL, NUM_EXPERTS), jnp.float32, -s_in, s_in), 'br': jax.random.uniform(ks[2], (NUM_EXPERTS,), jnp.float32, -s_in, s_in), 'W1': jax.random.uniform(ks[3], (NUM_EXPERTS, D_MODEL, D_FF), jnp.float32, -s_in, s_in), 'b1': jax.random.uniform(ks[4], (NUM_EXPERTS, D_FF), jnp.float32, -s_in, s_in), 'W2': jax.random.uniform(ks[5], (NUM_EXPERTS, D_FF, D_MODEL), jnp.float32, -s_ff, s_ff), 'b2': jax.random.uniform(ks[6], (NUM_EXPERTS, D_MODEL), jnp.float32, -s_ff, s_ff)}
    _L0_ffn_in = _L0_ffn_setup()
    _d = {'L0_attn_x': _L0_attn_in['x'], 'L0_attn_wq': _L0_attn_in['wq'], 'L0_attn_bq': _L0_attn_in['bq'], 'L0_attn_wk': _L0_attn_in['wk'], 'L0_attn_bk': _L0_attn_in['bk'], 'L0_attn_wv': _L0_attn_in['wv'], 'L0_attn_bv': _L0_attn_in['bv'], 'L0_attn_wo': _L0_attn_in['wo'], 'L0_attn_bo': _L0_attn_in['bo'], 'L0_ffn_Wr': _L0_ffn_in['Wr'], 'L0_ffn_br': _L0_ffn_in['br'], 'L0_ffn_W1': _L0_ffn_in['W1'], 'L0_ffn_b1': _L0_ffn_in['b1'], 'L0_ffn_W2': _L0_ffn_in['W2'], 'L0_ffn_b2': _L0_ffn_in['b2']}
    _x0 = _d['L0_attn_x']
    _d['L0_attn_x'] = jax.random.normal(jax.random.fold_in(jax.random.key(seed), 1), (4, 1024, 256), dtype=_x0.dtype)
    del _x0
    return _d

def reference(L0_attn_x, L0_attn_wq, L0_attn_bq, L0_attn_wk, L0_attn_bk, L0_attn_wv, L0_attn_bv, L0_attn_wo, L0_attn_bo, L0_ffn_Wr, L0_ffn_br, L0_ffn_W1, L0_ffn_b1, L0_ffn_W2, L0_ffn_b2):

    def _L0_attn_ref(x, wq, bq, wk, bk, wv, bv, wo, bo):
        import jax, jax.numpy as jnp
        import numpy as np
        B, T, D, H = (4, 512, 256, 16)
        HD = D // H
        NEG = -np.finfo(np.float32).max
        b, t, d = x.shape

        def proj(w, bias):
            y = x @ w + bias
            return y.reshape(b, t, H, HD).transpose(0, 2, 1, 3)
        q = proj(wq, bq)
        k = proj(wk, bk)
        v = proj(wv, bv)
        scale = 1.0 / np.sqrt(HD).astype(np.float32)
        scores = jnp.einsum('bhqd,bhkd->bhqk', q, k) * scale
        mask = jnp.triu(jnp.full((t, t), NEG, jnp.float32), k=1)
        attn = jax.nn.softmax(scores + mask, axis=-1)
        out = jnp.einsum('bhqk,bhkd->bhqd', attn, v)
        out = out.transpose(0, 2, 1, 3).reshape(b, t, d)
        return out @ wo + bo

    def _L0_ffn_ref(x, Wr, br, W1, b1, W2, b2):
        import jax, jax.numpy as jnp
        import numpy as np
        D_MODEL = 256
        D_FF = 1024
        NUM_EXPERTS = 8
        B, N = (16, 256)
        scores = jnp.einsum('bh,he->be', x.mean(axis=1), Wr) + br
        top1 = jnp.argmax(scores, axis=-1)
        w1 = W1[top1]
        c1 = b1[top1]
        w2 = W2[top1]
        c2 = b2[top1]
        h = jax.nn.relu(jnp.einsum('bnh,bhf->bnf', x, w1) + c1[:, None, :])
        out = jnp.einsum('bnf,bfh->bnh', h, w2) + c2[:, None, :]
        return out
    x = L0_attn_x
    x = _layernorm(x + _L0_attn_ref(x, L0_attn_wq, L0_attn_bq, L0_attn_wk, L0_attn_bk, L0_attn_wv, L0_attn_bv, L0_attn_wo, L0_attn_bo), axis=-1)
    x = _layernorm(x + _L0_ffn_ref(x, L0_ffn_Wr, L0_ffn_br, L0_ffn_W1, L0_ffn_b1, L0_ffn_W2, L0_ffn_b2), axis=-1)
    return x

_drawn_inputs = setup_inputs


def setup_inputs(seed=0):
    import zlib

    import numpy as np

    out = dict(_drawn_inputs(seed))
    spreads = {}
    factors = {'L0_attn_bq': 8.0,
     'L0_attn_bk': 64.0,
     'L0_attn_bo': 2.962,
     'L0_ffn_b1': 4.001,
     'L0_ffn_b2': 3.171,
     'L0_attn_bv': 2.737}
    for name, (base, spread) in spreads.items():
        noise = np.random.default_rng([zlib.crc32(name.encode()), seed]).standard_normal(out[name].shape)
        drawn = base * np.exp(spread * noise) if base else spread * noise
        out[name] = jnp.asarray(drawn.astype(out[name].dtype))
    for name, factor in factors.items():
        out[name] = (out[name] * factor).astype(out[name].dtype)
    return out
```

```python
from contextlib import ExitStack

import concourse.bass as bass
from concourse import mybir

F32 = mybir.dt.float32
BF16 = mybir.dt.bfloat16
U32 = mybir.dt.uint32
ALU = mybir.AluOpType
ACT = mybir.ActivationFunctionType
AX_X = mybir.AxisListType.X

P = 128
HD = 16
G = 4
BANK = 512
PARTS = 3
EPS = 1e-5
MASKED = -3.0e38
DMA_DONE = 16

ROWS3 = 3 * HD
ROWS2 = ROWS3 + 2 * HD
ROWS = ROWS2 + HD
ROWS_MAX = ROWS + PARTS

EXP_UNITS = [
    [(0, 0, 4, 0)], [(0, 4, 4, 0)], [(1, 4, 4, 0)], [(2, 4, 4, 0)], [(3, 4, 4, 0)], [(4, 4, 4, 0)],
    [(1, 1, 3, 0), (7, 7, 1, 3)], [(3, 3, 1, 0), (5, 5, 3, 1)], [(2, 2, 2, 0), (6, 6, 2, 2)],
]
MAX_UNITS = [
    [(4, 0, 4, 0)], [(5, 0, 4, 0)], [(6, 0, 4, 0)], [(7, 0, 4, 0)], [(3, 0, 4, 0)], [(7, 4, 4, 0)],
    [(2, 0, 3, 0), (4, 4, 1, 3)], [(0, 0, 1, 0), (6, 4, 3, 1)], [(1, 0, 2, 0), (5, 4, 2, 2)],
]
UNITS = len(EXP_UNITS)
PARTIAL = [(4, 1), (14, 1), (9, 1), (15, 1), (17, 1), (16, 1), (0, 4), (5, 4), (10, 4)]
PARTIALS = 18
PARTIAL_OF_BLOCK = [(5, 1), (10, 2), (0, 3), (17, 1), (3, 2), (12, 3), (6, 4), (15, 2)]
SLOTS = UNITS * G


class Signal:

    def __init__(self, sem, by=1):
        self.sem, self.by, self.count = sem, by, 0

    def mark(self):
        self.count += self.by
        return (self, self.count)


class Queue:

    def __init__(self):
        self.ops, self.waited = [], {}

    def wait(self, *tokens):
        for token in tokens:
            if token is None:
                continue
            signal, value = token
            if self.waited.get(signal, 0) < value:
                self.waited[signal] = value
                self.ops.append((None, signal.sem, value, None, None))

    def do(self, method, *args, signal=None, **kw):
        self.ops.append((method, args, kw, signal and signal.sem, signal and signal.by))
        return signal.mark() if signal else None

    def play(self, engine):
        for method, a, b, sem, by in self.ops:
            if method is None:
                engine.wait_ge(a, b)
            else:
                made = method(*a, **b)
                if sem is not None:
                    made.then_inc(sem, by)


def post_ln_layer(nc, x, xT, wq, wk, wv, bqkT, bv, wo, bo, wr, br, w1, b1T, w2, b2, out):
    B, T, D = x.shape
    E, _, F = w1.shape
    C = T // P
    M = D // P
    FC = F // P
    H = D // HD
    GROUPS = H // G
    PAIRS = GROUPS // 2
    HALVES = T // BANK
    CH = BANK // P
    LAST = B * GROUPS
    P_RING = 12
    SCALE = 1.0 / float(HD) ** 0.5

    with ExitStack() as ctx:
        def sb(name, shape, dt=F32):
            return ctx.enter_context(nc.sbuf_tensor(name, shape, dt))

        def ps(name, cols=BANK):
            return ctx.enter_context(nc.psum_tensor(name, [P, cols], F32))

        def sig(name, by=1):
            return Signal(ctx.enter_context(nc.semaphore(name)), by)

        identity = sb("identity", [P, P])
        identity_bf = sb("identity_bf", [P, P], BF16)
        causal = sb("causal", [P, P], BF16)
        wq_sb, wk_sb, wv_sb = (sb(n, [P, M, D]) for n in ("wq_sb", "wk_sb", "wv_sb"))
        wo_sb = sb("wo_sb", [P, PAIRS, D])
        wr_sb = sb("wr_sb", [P, M, E])
        bqk_sb = sb("bqk_sb", [P, 2, M])
        bv_sb, bo_sb, b2_sb = (sb(n, [P, D]) for n in ("bv_sb", "bo_sb", "b2_sb"))
        br_sb = sb("br_sb", [1, E])
        b1_sb = sb("b1_sb", [P, FC])
        xT_sb = sb("xT_sb", [P, M, T])
        parts = sb("parts", [P, 2, PARTS, T], BF16)
        part_rest = [sb(f"part_rest{i}", [P, BANK]) for i in range(2)]
        stack_q = [sb(f"stack_q{i}", [P, G, T], BF16) for i in range(3)]
        stack_k = [sb(f"stack_k{i}", [P, G, T], BF16) for i in range(3)]
        v_ones = sb("v_ones", [P, C, H, 2 * HD])
        partial_max = sb("partial_max", [P, G, PARTIALS])
        row_max = sb("row_max", [P, G, C])
        neg_max = sb("neg_max", [G * C, PARTS, P], BF16)
        neg_rest = sb("neg_rest", [G * C, P])
        prob = [sb(f"prob{i}", [P, BANK]) for i in range(P_RING)]
        o_sb = [sb(f"o_sb{i}", [P, T]) for i in range(2)]
        sums = sb("sums", [P, G * T // P])
        inv_sums = sb("inv_sums", [P, G * T // P])
        inv_rows = sb("inv_rows", [P, T])
        inv_wide = sb("inv_wide", [P, T])
        attn = sb("attn", [P, PAIRS, T])
        x1 = sb("x1", [P, C, D])
        x1T = sb("x1T", [P, M, T])
        x1_sum = sb("x1_sum", [P, M, HALVES])
        x1_mean = sb("x1_mean", [P, M])
        route = sb("route", [1, E])
        route_top = sb("route_top", [1, 8])
        route_at = sb("route_at", [1, 8], U32)
        w1_sb = sb("w1_sb", [P, M, F])
        w2_sb = sb("w2_sb", [P, FC, D])
        hidden = sb("hidden", [P, FC, BANK])
        ln_in = [sb(f"ln_in{i}", [P, 2, D]) for i in range(2)]
        ln_stats = [sb(f"ln_stats{i}", [P, 2, 6]) for i in range(2)]
        ln_mv = [sb(f"ln_mv{i}", [P, 2, 2]) for i in range(2)]
        ln_var = [sb(f"ln_var{i}", [P, 2]) for i in range(2)]
        ln_rstd = [sb(f"ln_rstd{i}", [P, 2]) for i in range(2)]
        minus_half = sb("minus_half", [P, 2])
        y_out = [sb(f"y_out{i}", [P, 2, D]) for i in range(2)]

        max_ps = [ps(f"max_ps{i}") for i in range(2)]
        exp_ps = [ps(f"exp_ps{i}") for i in range(2)]
        dense_ps = [ps(f"dense_ps{i}") for i in range(2)]
        o_ps = ps("o_ps", T)

        s_const = sig("s_const")
        s_ones = sig("s_ones")
        s_load = sig("s_load", DMA_DONE)
        s_xT = sig("s_xT", DMA_DONE)
        s_x = sig("s_x", DMA_DONE)
        s_w1, s_w2 = sig("s_w1", DMA_DONE), sig("s_w2", DMA_DONE)
        s_fill = [[sig(f"s_fill{i}_{c}", DMA_DONE) for c in range(G)] for i in range(3)]
        s_maxrow = [sig(f"s_maxrow{i}", DMA_DONE) for i in range(3)]
        s_sums, s_inv = sig("s_sums", DMA_DONE), sig("s_inv", DMA_DONE)
        s_out = [sig(f"s_out{i}", DMA_DONE) for i in range(2)]
        pe_max, pe_exp, pe_pv, pe_dense = sig("pe_max"), sig("pe_exp"), sig("pe_pv"), sig("pe_dense")
        dve_max, dve_row, dve_dense = sig("dve_max"), sig("dve_row"), sig("dve_dense")
        act_exp, act_o, act_dense = sig("act_exp"), sig("act_o"), sig("act_dense")
        pool_mask, pool_dense = sig("pool_mask"), sig("pool_dense")

        pe, act, dve, pool, sp = Queue(), Queue(), Queue(), Queue(), Queue()
        TE, VE, SE, GE, DMA = nc.tensor, nc.vector, nc.scalar, nc.gpsimd, nc.sync

        one = pool.do(GE.memset, identity[:, :], 0.0, signal=s_const)
        pool.do(GE.memset, causal[:, :], 0.0, signal=s_const)
        pool.do(GE.memset, inv_rows[:, :], 0.0, signal=s_const)
        pool.do(GE.memset, minus_half[:, :], -0.5, signal=s_const)
        zeroed = pool.do(GE.memset, v_ones[:, :, :, :], 1.0, signal=s_const)
        pool.wait(zeroed)
        t = pool.do(GE.affine_select, out=identity[:, :], in_=identity[:, :], compare_op=ALU.not_equal,
                    fill=1.0, base=0, pattern=[[-1, P]], channel_multiplier=1, signal=s_const)
        pool.do(GE.affine_select, out=causal[:, :], in_=causal[:, :], compare_op=ALU.is_ge,
                fill=MASKED, base=0, pattern=[[-1, P]], channel_multiplier=1, signal=s_const)
        pool.wait(t)
        constants = pool.do(GE.tensor_copy, identity_bf[:, :], identity[:, :], signal=s_const)

        for i in range(3):
            ones_rows = dve.do(VE.memset, stack_k[i][ROWS:ROWS_MAX, :, :], 1.0, signal=s_ones)

        def load(dst, src):
            return sp.do(DMA.dma_start, dst, src, signal=s_load)

        def load_xT(b):
            sp.wait(xT_read[0])
            return sp.do(DMA.dma_start, xT_sb[:, :, :], xT[b].rearrange("(m p) t -> p m t", p=P), signal=s_xT)

        xT_read = [None]
        xT_loaded = [None] * B
        xT_loaded[0] = load_xT(0)
        for dst, src in ((wq_sb, wq), (wk_sb, wk)):
            load(dst[:, :, :], src.rearrange("(m p) n -> p m n", p=P))
        qk_weights = load(bqk_sb[:, :, :], bqkT)
        load(wv_sb[:, :, :], wv.rearrange("(m p) n -> p m n", p=P))
        load(bv_sb[:, :], bv.partition_broadcast(P))
        load(wo_sb[:, :, :], wo.rearrange("(m p) n -> p m n", p=P))
        load(bo_sb[:, :], bo.partition_broadcast(P))
        load(wr_sb[:, :, :], wr.rearrange("(m p) n -> p m n", p=P))
        weights = load(br_sb[:, :], br)
        qk_weights = weights

        bank_read = [None, None]
        banks_taken = [0]

        def take_bank():
            n = banks_taken[0] % 2
            banks_taken[0] += 1
            pe.wait(bank_read[n])
            return n, dense_ps[n]

        now, deferred, serials = [0], [], iter(range(1 << 20))

        def later(slots, work, *args):
            deferred.append((now[0] + slots, next(serials), work, args))

        def run_deferred():
            while True:
                due = [d for d in deferred if d[0] <= now[0]]
                if not due:
                    return
                first = min(due)
                deferred.remove(first)
                first[2](*first[3])

        rest_read = [None, None]
        parts_done = {}
        fill_done = {}

        def qk_unit(p, which, half):
            b, m = p // PAIRS, p % PAIRS
            w_sb = (wq_sb, wk_sb)[which]
            pe.wait(qk_weights, xT_loaded[b])
            n, bank = take_bank()
            for j in range(M):
                done = pe.do(TE.matmul, bank[:, :], w_sb[:, j, m * P:(m + 1) * P],
                             xT_sb[:, j, half * BANK:(half + 1) * BANK], start=(j == 0), stop=(j == M - 1),
                             signal=pe_dense if j == M - 1 else None)
                if j < M - 1:
                    yield
            xT_read[0] = done
            later(1, split_parts, p, which, half, n, bank, done)
            yield

        def split_parts(p, which, half, n, bank, done):
            bias = bqk_sb[:, which, p % PAIRS:p % PAIRS + 1]
            part = [parts[:, which, i, half * BANK:(half + 1) * BANK] for i in range(PARTS)]
            if p > 0:
                act.wait(*fill_done[2 * p - 2], *fill_done[2 * p - 1])
                dve.wait(*fill_done[2 * p - 2], *fill_done[2 * p - 1])
                pool.wait(*fill_done[2 * p - 2], *fill_done[2 * p - 1])
            act.wait(done)
            first = act.do(SE.activation, part[0], bank[:, :], ACT.Identity, bias=bias, scale=1.0, signal=act_dense)
            k = half
            dve.wait(done, first, rest_read[k])
            rest = dve.do(VE.scalar_tensor_tensor, out=part_rest[k][:, :], in0=bank[:, :], scalar=bias,
                          in1=part[0], op0=ALU.add, op1=ALU.subtract, signal=dve_dense)
            bank_read[n] = rest
            dve.wait(rest)
            second = dve.do(VE.tensor_copy, part[1], part_rest[k][:, :], signal=dve_dense)
            pool.wait(second)
            third = pool.do(GE.tensor_tensor, part[2], part_rest[k][:, :], part[1], ALU.subtract, signal=pool_dense)
            rest_read[k] = third
            parts_done.setdefault(p, []).append(third)

        exp_read = {}

        def fill(g, c):
            slot, p = g % 3, g // 2
            lane = (g % 2) * G + c
            src = parts[lane * HD:(lane + 1) * HD, :, :, :]
            assert len(parts_done[p]) == 2 * HALVES
            sp.wait(parts_done[p][-1], exp_read.get(g - 3))
            q, k = stack_q[slot], stack_k[slot]
            for dst, a in (
                (k[0:ROWS3, c, :], src[:, 1, :, :]),
                (q[0:ROWS3, c, :], src[:, 0, 0:1, :].broadcast_to([HD, 3, T])),
                (k[ROWS3:ROWS2, c, :], src[:, 1, 0:2, :]),
                (q[ROWS3:ROWS2, c, :], src[:, 0, 1:2, :].broadcast_to([HD, 2, T])),
                (k[ROWS2:ROWS, c, :], src[:, 1, 0, :]),
                (q[ROWS2:ROWS, c, :], src[:, 0, 2, :]),
            ):
                done = sp.do(DMA.dma_start, dst, a, signal=s_fill[slot][c])
            fill_done.setdefault(g, []).append(done)

        v_done = {}

        def v_unit(b, t2):
            pe.wait(weights, xT_loaded[b])
            n, bank = take_bank()
            for i in range(2):
                for j in range(M):
                    tok = (2 * t2 + i) * P
                    done = pe.do(TE.matmul, bank[:, i * D:(i + 1) * D], xT_sb[:, j, tok:tok + P], wv_sb[:, j, :],
                                 start=(j == 0), stop=(j == M - 1), signal=pe_dense if i and j else None)
                if i == 0:
                    yield
            xT_read[0] = done
            later(1, v_store, b, t2, n, bank, done)
            yield

        def v_store(b, t2, n, bank, done):
            dve.wait(done, weights, constants, pv_done.get(b * GROUPS - 1))
            by_head = "p (r e c d) -> p r e c d"
            dims = dict(e=2, c=G, d=HD)
            bias = bv_sb[:, :].rearrange(by_head, **dims)
            for i in range(2):
                src = bank[:, i * D:(i + 1) * D].rearrange(by_head, **dims)
                dst = v_ones[:, 2 * t2 + i, :, :].rearrange("p (r e c) d -> p r e c d", e=2, c=G)
                for e in range(2):
                    t = dve.do(VE.tensor_tensor, dst[:, :, e, :, e * HD:(e + 1) * HD], src[:, :, e, :, :],
                               bias[:, :, e, :, :], ALU.add, signal=dve_dense)
            bank_read[n] = t
            v_done[b] = t

        max_done, row_read, neg_sent, maxrow_done = [], [None], [None], {}

        def max_unit(g, n):
            c, u = n // UNITS, n % UNITS
            slot, bank = g % 3, max_ps[n % 2]
            pe.wait(fill_done[g][c], constants)
            if len(max_done) >= 2:
                pe.wait(max_done[-2])
            for s, (i, k0, count, at) in enumerate(MAX_UNITS[u]):
                diagonal = k0 + count - 1 == i
                end = (at + count) * P
                final = s == len(MAX_UNITS[u]) - 1
                done = pe.do(TE.matmul, bank[:, at * P:end], stack_q[slot][0:ROWS, c, i * P:(i + 1) * P],
                             stack_k[slot][0:ROWS, c, k0 * P:(k0 + count) * P], start=True, stop=not diagonal,
                             signal=pe_max if final and not diagonal else None)
                if diagonal:
                    done = pe.do(TE.matmul, bank[:, end - P:end], identity_bf[:, :], causal[:, :],
                                 start=False, stop=True, signal=pe_max if final else None)
            first, count = PARTIAL[u]
            dve.wait(done)
            max_done.append(dve.do(VE.tensor_reduce, partial_max[:, c, first:first + count],
                                   bank[:, :].rearrange("p (a b) -> p a b", a=count), AX_X, ALU.max,
                                   signal=dve_max))

        def max_rows(g):
            dve.wait(max_done[-1], row_read[0])
            for i, (first, count) in enumerate(PARTIAL_OF_BLOCK):
                done = dve.do(VE.tensor_reduce, row_max[:, :, i], partial_max[:, :, first:first + count],
                              AX_X, ALU.max, signal=dve_row)
            later(1, max_turn, g, done)

        def max_turn(g, done):
            pe.wait(done, constants)
            n, bank = take_bank()
            done = pe.do(TE.transpose, bank[0:G * C, 0:P], row_max[:, :, :].rearrange("p c i -> p (c i)"),
                         identity[:, :], signal=pe_dense)
            row_read[0] = done
            rows = bank[0:G * C, 0:P]
            dve.wait(done, neg_sent[0])
            t = dve.do(VE.tensor_scalar, neg_max[:, 0, :], rows, -1.0, None, ALU.mult, signal=dve_dense)
            dve.wait(t)
            t = dve.do(VE.scalar_tensor_tensor, out=neg_rest[:, :], in0=rows, scalar=-1.0, in1=neg_max[:, 0, :],
                       op0=ALU.mult, op1=ALU.subtract, signal=dve_dense)
            bank_read[n] = t
            dve.wait(t)
            t = dve.do(VE.tensor_copy, neg_max[:, 1, :], neg_rest[:, :], signal=dve_dense)
            dve.wait(t)
            t = dve.do(VE.tensor_tensor, neg_max[:, 2, :], neg_rest[:, :], neg_max[:, 1, :], ALU.subtract,
                       signal=dve_dense)
            sp.wait(t, exp_read.get(g - 3))
            for i in range(PARTS):
                t = sp.do(DMA.dma_start, stack_q[g % 3][ROWS + i:ROWS + i + 1, :, :].rearrange("p c t -> p (c t)"),
                          neg_max[:, i, :], signal=s_maxrow[g % 3])
            neg_sent[0] = maxrow_done[g] = t

        exp_done, prob_done, pv_done, pv_of_set = [], [], {}, []

        def exp_unit(g, n):
            u, c = n // G, n % G
            slot, serial = g % 3, g * SLOTS + n
            bank, p_sb = exp_ps[serial % 2], prob[serial % P_RING]
            pe.wait(maxrow_done[g], ones_rows)
            if serial >= 2:
                pe.wait(exp_done[serial - 2])
            for s, (j, q0, count, at) in enumerate(EXP_UNITS[u]):
                final = s == len(EXP_UNITS[u]) - 1
                done = pe.do(TE.matmul, bank[:, at * P:(at + count) * P],
                             stack_k[slot][0:ROWS_MAX, c, j * P:(j + 1) * P],
                             stack_q[slot][0:ROWS_MAX, c, q0 * P:(q0 + count) * P], start=True, stop=True,
                             signal=pe_exp if final else None)
            exp_read[g] = done
            act.wait(done)
            if serial >= P_RING:
                act.wait(pv_of_set[(serial - P_RING) // G])
            t = act.do(SE.activation, p_sb[:, :], bank[:, :], ACT.Exp, scale=SCALE, signal=act_exp)
            exp_done.append(t)
            for j, q0, count, at in EXP_UNITS[u]:
                if j == q0:
                    pool.wait(exp_done[serial])
                    block = p_sb[:, at * P:(at + 1) * P]
                    t = pool.do(GE.affine_select, out=block, in_=block, compare_op=ALU.is_ge, fill=0.0, base=0,
                                pattern=[[1, P]], channel_multiplier=-1, signal=pool_mask)
            prob_done.append(t)

        o_read = [None]

        def pv_set(g, u):
            first = g * SLOTS + u * G
            b, h0 = g // GROUPS, (g % GROUPS) * G
            pe.wait(v_done[b])
            if u == 0:
                pe.wait(o_read[0])
            final = u == UNITS - 1
            for s, (j, q0, count, at) in enumerate(EXP_UNITS[u]):
                for c in range(G):
                    if s == 0:
                        pe.wait(prob_done[first + c])
                    end = s == len(EXP_UNITS[u]) - 1 and c == G - 1
                    done = pe.do(TE.matmul, o_ps[32 * c:32 * c + 32, q0 * P:(q0 + count) * P],
                                 v_ones[:, j, h0 + c, :], prob[(first + c) % P_RING][:, at * P:(at + count) * P],
                                 start=(u < 2), stop=final, signal=pe_pv if end else None)
            pv_of_set.append(done)
            if final:
                pv_done[g] = done
                later(1, o_store, g)

        scaled_read = [None, None]
        inv_rows_read, inv_wide_read, attn_read, attn_done = [None], [None], [None], {}

        def o_store(g):
            e = g % 2
            act.wait(pv_done[g], scaled_read[e])
            t = act.do(SE.copy, o_sb[e][:, :], o_ps[:, :], signal=act_o)
            o_read[0] = t
            first = HD * (1 - e)
            sp.wait(t)
            for c in range(G):
                row = 32 * c + first
                t = sp.do(DMA.dma_start, sums[32 * c:32 * c + 32, :], o_sb[e][row:row + 1, :], signal=s_sums)
            later(3, invert, g, t)

        def invert(g, t):
            dve.wait(t)
            t = dve.do(VE.reciprocal, inv_sums[:, :], sums[:, :], signal=dve_dense)
            sp.wait(t, inv_rows_read[0], constants)
            for c in range(G):
                t = sp.do(DMA.dma_start, inv_rows[32 * c:32 * c + 1, :], inv_sums[32 * c:32 * c + 32, :], signal=s_inv)
            later(3, spread, g, t)

        def spread(g, t):
            e, r = g % 2, (g % GROUPS) // 2
            mask = [1] * 32
            mask[e * HD:(e + 1) * HD] = [0] * HD
            dve.wait(t, inv_wide_read[0])
            t = dve.do(VE.stream_shuffle, inv_wide[:, :], inv_rows[:, :], mask, signal=dve_dense)
            inv_rows_read[0] = t
            pool.wait(t)
            if e == 0:
                pool.wait(attn_read[0] if r == 0 else None)
                t = pool.do(GE.tensor_tensor, attn[:, r, :], o_sb[0][:, :], inv_wide[:, :], ALU.mult, signal=pool_dense)
            else:
                t = pool.do(GE.tensor_tensor, o_sb[1][:, :], o_sb[1][:, :], inv_wide[:, :], ALU.mult, signal=pool_dense)
            inv_wide_read[0] = t
            if e == 1:
                pool.wait(t)
                t = pool.do(GE.tensor_tensor, attn[:, r, :], attn[:, r, :], o_sb[1][:, :], ALU.add, signal=pool_dense)
            scaled_read[e] = t
            attn_done[g] = t

        ln_turn, ln_open = [0], [False, False]

        def layer_norm(bank, n, residual, outs, before, finish):
            k = ln_turn[0] % 2
            ln_turn[0] += 1
            assert not ln_open[k]
            ln_open[k] = True
            y, stats, mv = ln_in[k], ln_stats[k], ln_mv[k]
            dve.wait(*before)
            t = dve.do(VE.tensor_tensor, y[:, :, :], bank[:, :].rearrange("p (i d) -> p i d", i=2), residual,
                       ALU.add, signal=dve_dense)
            bank_read[n] = t
            dve.wait(t)
            for i in range(2):
                t = dve.do(VE.bn_stats, stats[:, i, :], y[:, i, :], signal=dve_dense)
            dve.wait(t)
            for i in range(2):
                t = dve.do(VE.bn_aggr, mv[:, i, :], stats[:, i, :], signal=dve_dense)
            dve.wait(t)
            t = dve.do(VE.tensor_scalar, ln_var[k][:, :], mv[:, :, 1], EPS, None, ALU.add, signal=dve_dense)
            pool.wait(t, constants)
            t = pool.do(GE.tensor_tensor, ln_rstd[k][:, :], ln_var[k][:, :], minus_half[:, :], ALU.pow,
                        signal=pool_dense)
            later(2, normalise, k, outs, t, finish)

        def normalise(k, outs, t, finish):
            ln_open[k] = False
            dve.wait(t)
            for i in range(2):
                t = dve.do(VE.tensor_scalar, outs[i], ln_in[k][:, i, :], ln_mv[k][:, i, 0:1], ln_rstd[k][:, i:i + 1],
                           ALU.subtract, ALU.mult, signal=dve_dense)
            finish(t)

        x_loaded, x_ready, x1_free, x1_done = {}, {}, [None], {}

        def load_x(b):
            sp.wait(x1_free[0])
            t = sp.do(DMA.dma_start, x1[:, :, :], x[b].rearrange("(c p) d -> p c d", p=P), signal=s_x)
            later(4, add_bo, b, t)

        def add_bo(b, t):
            pool.wait(t, weights)
            x_ready[b] = pool.do(GE.tensor_tensor, x1[:, :, :], x1[:, :, :],
                                 bo_sb[:, :].rearrange("p (o d) -> p o d", o=1).broadcast_to([P, C, D]),
                                 ALU.add, signal=pool_dense)

        def wo_unit(b, t2):
            pe.wait(weights, attn_done[(b + 1) * GROUPS - 1])
            n, bank = take_bank()
            for i in range(2):
                tok = (2 * t2 + i) * P
                for r in range(PAIRS):
                    done = pe.do(TE.matmul, bank[:, i * D:(i + 1) * D], attn[:, r, tok:tok + P], wo_sb[:, r, :],
                                 start=(r == 0), stop=(r == PAIRS - 1), signal=pe_dense if i and r else None)
                if i == 0:
                    yield
            attn_read[0] = done
            later(1, ln1, b, t2, n, bank, done)
            yield

        def ln1(b, t2, n, bank, done):
            rows = x1[:, 2 * t2:2 * t2 + 2, :]

            def finish(t):
                x1_done[(b, t2)] = t

            layer_norm(bank, n, rows, [rows[:, 0, :], rows[:, 1, :]], [done, x_ready[b]], finish)

        x1T_done, x1T_free, x1_turned = {}, [None], {}

        def turn_unit(b, half, m):
            pe.wait(x1_done[(b, 2 * half)], x1_done[(b, 2 * half + 1)], constants)
            n, bank = take_bank()
            for i in range(CH):
                done = pe.do(TE.transpose, bank[:, i * P:(i + 1) * P],
                             x1[:, half * CH + i, m * P:(m + 1) * P], identity[:, :],
                             signal=pe_dense if i == CH - 1 else None)
            x1_turned[b] = done
            later(1, turn_store, b, half, m, n, bank, done)
            yield

        def turn_store(b, half, m, n, bank, done):
            act.wait(done, x1T_free[0])
            t = act.do(SE.activation, x1T[:, m, half * BANK:(half + 1) * BANK], bank[:, :], ACT.Copy,
                       accum_out=x1_sum[:, m, half:half + 1], signal=act_dense)
            bank_read[n] = t
            x1T_done[(b, half)] = t

        w_free, w1_loaded, w2_loaded, b2_added = [None], {}, {}, {}

        def route_unit(b):
            dve.wait(x1T_done[(b, HALVES - 1)])
            t = dve.do(VE.tensor_reduce, x1_mean[:, :], x1_sum[:, :, :], AX_X, ALU.add, signal=dve_dense)
            pe.wait(t, weights)
            n, bank = take_bank()
            for m in range(M):
                done = pe.do(TE.matmul, bank[0:1, 0:E], x1_mean[:, m:m + 1], wr_sb[:, m, :], start=(m == 0),
                             stop=(m == M - 1), signal=pe_dense if m == M - 1 else None)
            later(1, pick, b, n, bank, done)
            yield

        def pick(b, n, bank, done):
            dve.wait(done, weights)
            t = dve.do(VE.scalar_tensor_tensor, out=route[:, :], in0=bank[0:1, 0:E], scalar=1.0 / T,
                       in1=br_sb[:, :], op0=ALU.mult, op1=ALU.add, signal=dve_dense)
            bank_read[n] = t
            dve.wait(t)
            t = dve.do(VE.max, route_top[:, :], route[:, :], signal=dve_dense)
            dve.wait(t, w2_loaded.get(b - 1))
            t = dve.do(VE.max_index, route_at[:, :], route_top[:, :], route[:, :], signal=dve_dense)
            later(2, load_expert, b, t)

        def load_expert(b, t):
            sp.wait(t, w_free[0])

            def issue(kind):
                if kind == 0:
                    expert = nc.sync.value_load(route_at[0:1, 0:1], min_val=0, max_val=E - 1)
                    issue.expert = expert
                    return nc.sync.dma_start(w1_sb[:, :, :],
                                             w1[bass.ds(expert, 1), :, :].rearrange("e (m p) f -> p (e m) f", p=P))
                if kind == 1:
                    return nc.sync.dma_start(b1_sb[:, :],
                                             b1T[bass.ds(issue.expert, 1), :, :].rearrange("e p f -> p (e f)"))
                if kind == 2:
                    return nc.sync.dma_start(w2_sb[:, :, :],
                                             w2[bass.ds(issue.expert, 1), :, :].rearrange("e (m p) d -> p (e m) d", p=P))
                return nc.sync.dma_start(b2_sb[:, :], b2[bass.ds(issue.expert, 1), :].broadcast_to([P, D]))

            for kind, signal in ((0, s_w1), (1, s_w1), (2, s_w2), (3, s_w2)):
                t = sp.do(issue, kind, signal=signal)
                (w1_loaded if kind < 2 else w2_loaded)[b] = t
            later(6, add_b2, b)

        def add_b2(b):
            pool.wait(w2_loaded[b], x1_turned[b])
            b2_added[b] = pool.do(GE.tensor_tensor, x1[:, :, :], x1[:, :, :],
                                  b2_sb[:, :].rearrange("p (o d) -> p o d", o=1).broadcast_to([P, C, D]),
                                  ALU.add, signal=pool_dense)

        hidden_done, hidden_free = {}, [None]

        def ffn1_unit(b, half, f):
            pe.wait(w1_loaded[b], x1T_done[(b, half)])
            n, bank = take_bank()
            for m in range(M):
                done = pe.do(TE.matmul, bank[:, :], w1_sb[:, m, f * P:(f + 1) * P],
                             x1T[:, m, half * BANK:(half + 1) * BANK], start=(m == 0), stop=(m == M - 1),
                             signal=pe_dense if m == M - 1 else None)
                if m < M - 1:
                    yield
            if f == FC - 1 and half == HALVES - 1:
                x1T_free[0] = done
            later(1, relu, b, half, f, n, bank, done)
            yield

        def relu(b, half, f, n, bank, done):
            act.wait(done, hidden_free[0])
            t = act.do(SE.activation, hidden[:, f, :], bank[:, :], ACT.Relu, bias=b1_sb[:, f:f + 1], scale=1.0,
                       signal=act_dense)
            bank_read[n] = t
            hidden_done[(b, half)] = t

        def ffn2_unit(b, half, t2):
            pe.wait(w2_loaded[b], hidden_done[(b, half)])
            n, bank = take_bank()
            for i in range(2):
                tok = (2 * t2 + i) * P
                for f in range(FC):
                    done = pe.do(TE.matmul, bank[:, i * D:(i + 1) * D], hidden[:, f, tok:tok + P], w2_sb[:, f, :],
                                 start=(f == 0), stop=(f == FC - 1),
                                 signal=pe_dense if i and f == FC - 1 else None)
                    if f % 2 and not (i and f == FC - 1):
                        yield
            if t2 == CH // 2 - 1:
                hidden_free[0] = done
                if half == HALVES - 1:
                    w_free[0] = done
            later(1, ln2, b, half, t2, n, bank, done)
            yield

        y_sent = [None, None]

        def ln2(b, half, t2, n, bank, done):
            blocks = half * CH + 2 * t2
            k = (blocks // 2) % 2
            y = y_out[k]

            def finish(t):
                rows = out[b].rearrange("(c p) d -> p c d", p=P)
                sp.wait(t)
                y_sent[k] = sp.do(DMA.dma_start, rows[:, blocks:blocks + 2, :], y[:, :, :], signal=s_out[k])

            layer_norm(bank, n, x1[:, blocks:blocks + 2, :], [y[:, 0, :], y[:, 1, :]],
                       [done, b2_added[b], y_sent[k]], finish)
            x1_free[0] = bank_read[n]

        def dense_work(step):
            work = []
            b, r = step // GROUPS, step % GROUPS
            p = step // 2 + 1
            if step < 0:
                b, r = None, None
            if step >= 0 and r == 0 and b < B:
                work += [(3, 2, v_unit(b, t2), True) for t2 in range(C // 2)]
            if step % 2 == 0 and p < B * PAIRS:
                work += [(3, M, qk_unit(p, w, half), True) for half in range(HALVES) for w in range(2)]
            if step >= GROUPS:
                d = b - 1
                if r == 0:
                    work += [(15, 2, wo_unit(d, t2), False) for t2 in range(C // 2)]
                    work += [(22, 1, turn_unit(d, half, m), False) for half in range(HALVES) for m in range(M)]
                    work += [(27, 1, route_unit(d), False)]
                if r == 1:
                    work += [(4, M, ffn1_unit(d, 0, f), False) for f in range(FC)]
                    work += [(4, FC, ffn2_unit(d, 0, t2), False) for t2 in range(CH // 2)]
                if r == 2:
                    work += [(0, M, ffn1_unit(d, 1, f), False) for f in range(FC)]
                if r == 3:
                    work += [(0, FC, ffn2_unit(d, 1, t2), False) for t2 in range(CH // 2)]
            return work

        def run_pieces(work, slot):
            left = sum(w[1] for w in work)
            share = -(-left // (SLOTS - slot))
            if work and work[0][3]:
                share = max(share, 2)
            while share > 0 and work and work[0][0] <= slot:
                first, pieces, unit, urgent = work[0]
                next(unit)
                share -= 1
                work[0] = (first, pieces - 1, unit, urgent)
                if pieces == 1:
                    work.pop(0)

        for step in range(-2, LAST + GROUPS):
            work = dense_work(step)
            b = step // GROUPS
            fill_group = step + 2
            fill_from = 14 if step % 2 == 0 else 1
            for slot in range(SLOTS):
                now[0] = (step + 2) * SLOTS + slot
                run_deferred()
                if 0 <= step < LAST:
                    exp_unit(step, slot)
                if 0 <= step + 1 < LAST:
                    for n in range(slot * 3 // 2, min(SLOTS, (slot + 1) * 3 // 2)):
                        max_unit(step + 1, n)
                        if n == SLOTS - 1:
                            max_rows(step + 1)
                run_pieces(work, slot)
                if 0 <= step < LAST and slot % G == 2 and slot > G:
                    pv_set(step, slot // G - 1)
                if 0 < step <= LAST and slot == 2:
                    pv_set(step - 1, UNITS - 1)
                if fill_group < LAST and slot >= fill_from and (slot - fill_from) % 5 == 0:
                    c = (slot - fill_from) // 5
                    if c < G:
                        fill(fill_group, c)
                if step > 0 and step % GROUPS == 0 and slot == 4:
                    load_x(b - 1)
                if step >= 0 and step % GROUPS == 0 and slot == 20 and b + 1 < B:
                    xT_loaded[b + 1] = load_xT(b + 1)
            assert not work
        for _ in range(100):
            now[0] += 1
            run_deferred()
        assert not deferred
        sp.wait(*y_sent)

        block = ctx.enter_context(nc.Block())

        @block.tensor
        def _(engine):
            pe.play(engine)

        @block.vector
        def _(engine):
            dve.play(engine)

        @block.scalar
        def _(engine):
            act.play(engine)

        @block.gpsimd
        def _(engine):
            pool.play(engine)

        @block.sync
        def _(engine):
            sp.play(engine)


def kernel(L0_attn_x, L0_attn_wq, L0_attn_bq, L0_attn_wk, L0_attn_bk, L0_attn_wv, L0_attn_bv, L0_attn_wo,
           L0_attn_bo, L0_ffn_Wr, L0_ffn_br, L0_ffn_W1, L0_ffn_b1, L0_ffn_W2, L0_ffn_b2):
    import numpy as np
    import concourse.bacc as bacc
    from concourse.bass_utils import run_bass_kernel_spmd

    x = np.asarray(L0_attn_x)
    D = x.shape[-1]
    E = L0_ffn_W1.shape[0]
    wo = np.asarray(L0_attn_wo).reshape(D // P, 2, G, HD, D).transpose(0, 2, 1, 3, 4).reshape(D, D)
    bqkT = np.stack([np.asarray(L0_attn_bq).reshape(-1, P).T, np.asarray(L0_attn_bk).reshape(-1, P).T], axis=1)
    layouts = {
        "x": x, "xT": x.transpose(0, 2, 1),
        "wq": L0_attn_wq, "wk": L0_attn_wk, "wv": L0_attn_wv, "bqkT": bqkT,
        "bv": np.asarray(L0_attn_bv).reshape(1, -1), "wo": wo, "bo": np.asarray(L0_attn_bo).reshape(1, -1),
        "wr": L0_ffn_Wr, "br": np.asarray(L0_ffn_br).reshape(1, -1),
        "w1": L0_ffn_W1, "b1T": np.asarray(L0_ffn_b1).reshape(E, -1, P).transpose(0, 2, 1),
        "w2": L0_ffn_W2, "b2": L0_ffn_b2,
    }
    nc = bacc.Bacc("TRN2", target_bir_lowering=False, num_devices=1)
    arrays, args = {}, []
    for name, a in layouts.items():
        a = np.ascontiguousarray(a)
        arrays[f"in_{name}"] = a
        args.append(nc.dram_tensor(f"in_{name}", a.shape, mybir.dt.from_np(a.dtype), kind="ExternalInput").ap())
    out = nc.dram_tensor("out", x.shape, mybir.dt.from_np(x.dtype), kind="ExternalOutput").ap()
    post_ln_layer(nc, *args, out)
    r = run_bass_kernel_spmd(nc, [arrays], core_ids=[0])
    return r.results[0]["out"]
```

```python
from contextlib import ExitStack

import concourse.bass as bass
from concourse import mybir

F32 = mybir.dt.float32
BF16 = mybir.dt.bfloat16
U32 = mybir.dt.uint32
ALU = mybir.AluOpType
ACT = mybir.ActivationFunctionType
AX_X = mybir.AxisListType.X

P = 128
HD = 16
G = 4
BANK = 512
PARTS = 3
EPS = 1e-5
MASKED = -3.0e38
DMA_DONE = 16

ROWS3 = 3 * HD
ROWS2 = ROWS3 + 2 * HD
ROWS = ROWS2 + HD
ROWS_MAX = ROWS + PARTS

EXP_UNITS = [
    [(0, 0, 4, 0)], [(0, 4, 4, 0)], [(1, 4, 4, 0)], [(2, 4, 4, 0)], [(3, 4, 4, 0)], [(4, 4, 4, 0)],
    [(1, 1, 3, 0), (7, 7, 1, 3)], [(3, 3, 1, 0), (5, 5, 3, 1)], [(2, 2, 2, 0), (6, 6, 2, 2)],
]
MAX_UNITS = [
    [(4, 0, 4, 0)], [(5, 0, 4, 0)], [(6, 0, 4, 0)], [(7, 0, 4, 0)], [(3, 0, 4, 0)], [(7, 4, 4, 0)],
    [(2, 0, 3, 0), (4, 4, 1, 3)], [(0, 0, 1, 0), (6, 4, 3, 1)], [(1, 0, 2, 0), (5, 4, 2, 2)],
]
UNITS = len(EXP_UNITS)
PARTIAL = [(4, 1), (14, 1), (9, 1), (15, 1), (17, 1), (16, 1), (0, 4), (5, 4), (10, 4)]
PARTIALS = 18
PARTIAL_OF_BLOCK = [(5, 1), (10, 2), (0, 3), (17, 1), (3, 2), (12, 3), (6, 4), (15, 2)]
SLOTS = UNITS * G
MAX_SLOTS = 31
NEAR = 60


class Signal:

    def __init__(self, sem, by=1):
        self.sem, self.by, self.count = sem, by, 0

    def mark(self, at):
        self.count += self.by
        return (self, self.count, at)


class Queue:

    def __init__(self, price, latency):
        self.ops, self.waited, self.clock, self.price, self.latency = [], {}, 0.0, price, latency

    def wait(self, *tokens):
        for token in tokens:
            if token is None:
                continue
            signal, value, at = token
            self.clock = max(self.clock, at)
            if self.waited.get(signal, 0) < value:
                self.waited[signal] = value
                self.ops.append((None, signal.sem, value, None, None))

    def do(self, method, *args, signal=None, ns=None, **kw):
        self.ops.append((method, args, kw, signal and signal.sem, signal and signal.by))
        self.clock += self.price(args, kw) if ns is None else ns
        return signal.mark(self.clock + self.latency) if signal else None

    def play(self, engine):
        for method, a, b, sem, by in self.ops:
            if method is None:
                engine.wait_ge(a, b)
            else:
                made = method(*a, **b)
                if sem is not None:
                    made.then_inc(sem, by)


def columns(args, kw):
    found = [a for a in (*args[:2], kw.get("out"), kw.get("in_"), kw.get("in0")) if isinstance(a, bass.AP)]
    return max(a.free_size() for a in found)


def pe_price(args, kw):
    moving = args[2]
    passes = 4 if moving.dtype == F32 and args[0].free_size() > P else 1
    return passes * (moving.free_size() / 2.4 + 3)


def act_price(args, kw):
    return 60 + columns(args, kw) / 1.2 + (93 if "bias" in kw else 0)


def dve_price(args, kw):
    return 66 + columns(args, kw) / 0.96


def pool_price(args, kw):
    return 90 + columns(args, kw) * (1.2 if "pattern" in kw else 2.2)


def dma_price(args, kw):
    return 620


def post_ln_layer(nc, x, xT, wq, wk, wv, bqkT, bv, wo, bo, wr, br, w1, b1T, w2, b2, out):
    B, T, D = x.shape
    E, _, F = w1.shape
    C = T // P
    M = D // P
    FC = F // P
    H = D // HD
    GROUPS = H // G
    PAIRS = GROUPS // 2
    HALVES = T // BANK
    CH = BANK // P
    LAST = B * GROUPS
    P_RING = 12
    SCALE = 1.0 / float(HD) ** 0.5

    with ExitStack() as ctx:
        def sb(name, shape, dt=F32):
            return ctx.enter_context(nc.sbuf_tensor(name, shape, dt))

        def ps(name, cols=BANK):
            return ctx.enter_context(nc.psum_tensor(name, [P, cols], F32))

        def sig(name, by=1):
            return Signal(ctx.enter_context(nc.semaphore(name)), by)

        identity = sb("identity", [P, P])
        identity_bf = sb("identity_bf", [P, P], BF16)
        causal = sb("causal", [P, P], BF16)
        wq_sb, wk_sb, wv_sb = (sb(n, [P, M, D]) for n in ("wq_sb", "wk_sb", "wv_sb"))
        wo_sb = sb("wo_sb", [P, PAIRS, D])
        wr_sb = sb("wr_sb", [P, M, E])
        bqk_sb = sb("bqk_sb", [P, 2, M])
        bv_sb, bo_sb, b2_sb = (sb(n, [P, D]) for n in ("bv_sb", "bo_sb", "b2_sb"))
        br_sb = sb("br_sb", [1, E])
        b1_sb = sb("b1_sb", [P, FC])
        xT_sb = sb("xT_sb", [P, M, T])
        parts = sb("parts", [P, 2, PARTS, T], BF16)
        part_rest = [sb(f"part_rest{i}", [P, BANK]) for i in range(2)]
        stack_q = [sb(f"stack_q{i}", [P, G, T], BF16) for i in range(3)]
        stack_k = [sb(f"stack_k{i}", [P, G, T], BF16) for i in range(3)]
        v_ones = sb("v_ones", [P, C, H, 2 * HD])
        partial_max = sb("partial_max", [P, G, PARTIALS])
        row_max = sb("row_max", [P, G, C])
        neg_max = sb("neg_max", [G * C, PARTS, P], BF16)
        neg_rest = sb("neg_rest", [G * C, P])
        prob = [sb(f"prob{i}", [P, BANK]) for i in range(P_RING)]
        o_sb = [sb(f"o_sb{i}", [P, T]) for i in range(2)]
        sums = sb("sums", [P, G * T // P])
        inv_sums = sb("inv_sums", [P, G * T // P])
        inv_rows = sb("inv_rows", [P, T])
        inv_wide = sb("inv_wide", [P, T])
        attn = sb("attn", [P, PAIRS, T])
        x1 = sb("x1", [P, C, D])
        x1T = sb("x1T", [P, M, T])
        x1_sum = sb("x1_sum", [P, M, HALVES])
        x1_mean = sb("x1_mean", [P, M])
        route = sb("route", [1, E])
        route_top = sb("route_top", [1, 8])
        route_at = sb("route_at", [1, 8], U32)
        w1_sb = sb("w1_sb", [P, M, F])
        w2_sb = sb("w2_sb", [P, FC, D])
        hidden = sb("hidden", [P, FC, BANK])
        ln_in = [sb(f"ln_in{i}", [P, 2, D]) for i in range(2)]
        ln_stats = [sb(f"ln_stats{i}", [P, 2, 6]) for i in range(2)]
        ln_mv = [sb(f"ln_mv{i}", [P, 2, 2]) for i in range(2)]
        ln_var = [sb(f"ln_var{i}", [P, 2]) for i in range(2)]
        ln_rstd = [sb(f"ln_rstd{i}", [P, 2]) for i in range(2)]
        minus_half = sb("minus_half", [P, 2])
        y_out = [sb(f"y_out{i}", [P, 2, D]) for i in range(2)]

        max_ps = [ps(f"max_ps{i}") for i in range(2)]
        exp_ps = [ps(f"exp_ps{i}") for i in range(2)]
        dense_ps = [ps(f"dense_ps{i}") for i in range(2)]
        o_ps = ps("o_ps", T)

        s_const = sig("s_const")
        s_ones = sig("s_ones")
        s_load = sig("s_load", DMA_DONE)
        s_xT = sig("s_xT", DMA_DONE)
        s_x = sig("s_x", DMA_DONE)
        s_w1, s_w2 = sig("s_w1", DMA_DONE), sig("s_w2", DMA_DONE)
        s_fill = [[sig(f"s_fill{i}_{c}", DMA_DONE) for c in range(G)] for i in range(3)]
        s_maxrow = [sig(f"s_maxrow{i}", DMA_DONE) for i in range(3)]
        s_sums, s_inv = sig("s_sums", DMA_DONE), sig("s_inv", DMA_DONE)
        s_out = [sig(f"s_out{i}", DMA_DONE) for i in range(2)]
        pe_max, pe_exp, pe_pv, pe_dense = sig("pe_max"), sig("pe_exp"), sig("pe_pv"), sig("pe_dense")
        dve_max, dve_row, dve_dense = sig("dve_max"), sig("dve_row"), sig("dve_dense")
        act_exp, act_o, act_dense = sig("act_exp"), sig("act_o"), sig("act_dense")
        pool_mask, pool_dense = sig("pool_mask"), sig("pool_dense")

        pe, act, dve = Queue(pe_price, 230), Queue(act_price, 70), Queue(dve_price, 70)
        pool, sp = Queue(pool_price, 100), Queue(dma_price, 1900)
        TE, VE, SE, GE, DMA = nc.tensor, nc.vector, nc.scalar, nc.gpsimd, nc.sync

        one = pool.do(GE.memset, identity[:, :], 0.0, signal=s_const)
        pool.do(GE.memset, causal[:, :], 0.0, signal=s_const)
        pool.do(GE.memset, inv_rows[:, :], 0.0, signal=s_const)
        pool.do(GE.memset, minus_half[:, :], -0.5, signal=s_const)
        zeroed = pool.do(GE.memset, v_ones[:, :, :, :], 1.0, signal=s_const)
        pool.wait(zeroed)
        t = pool.do(GE.affine_select, out=identity[:, :], in_=identity[:, :], compare_op=ALU.not_equal,
                    fill=1.0, base=0, pattern=[[-1, P]], channel_multiplier=1, signal=s_const)
        pool.do(GE.affine_select, out=causal[:, :], in_=causal[:, :], compare_op=ALU.is_ge,
                fill=MASKED, base=0, pattern=[[-1, P]], channel_multiplier=1, signal=s_const)
        pool.wait(t)
        constants = pool.do(GE.tensor_copy, identity_bf[:, :], identity[:, :], signal=s_const)

        for i in range(3):
            ones_rows = dve.do(VE.memset, stack_k[i][ROWS:ROWS_MAX, :, :], 1.0, signal=s_ones)

        def load(dst, src):
            return sp.do(DMA.dma_start, dst, src, signal=s_load)

        def load_xT(b):
            sp.wait(xT_read[0])
            return sp.do(DMA.dma_start, xT_sb[:, :, :], xT[b].rearrange("(m p) t -> p m t", p=P), signal=s_xT)

        xT_read = [None]
        xT_loaded = [None] * B
        xT_loaded[0] = load_xT(0)
        for dst, src in ((wq_sb, wq), (wk_sb, wk)):
            load(dst[:, :, :], src.rearrange("(m p) n -> p m n", p=P))
        qk_weights = load(bqk_sb[:, :, :], bqkT)
        load(wv_sb[:, :, :], wv.rearrange("(m p) n -> p m n", p=P))
        load(bv_sb[:, :], bv.partition_broadcast(P))
        load(wo_sb[:, :, :], wo.rearrange("(m p) n -> p m n", p=P))
        load(bo_sb[:, :], bo.partition_broadcast(P))
        load(wr_sb[:, :, :], wr.rearrange("(m p) n -> p m n", p=P))
        weights = load(br_sb[:, :], br)
        qk_weights = weights

        bank_read = [None, None]
        bank_open = [False, False]
        banks_taken = [0]

        def bank_ready():
            return not bank_open[banks_taken[0] % 2]

        def take_bank():
            n = banks_taken[0] % 2
            banks_taken[0] += 1
            assert not bank_open[n]
            pe.wait(bank_read[n])
            bank_open[n] = True
            return n, dense_ps[n]

        def bank_was_read(n, token):
            bank_read[n], bank_open[n] = token, False

        deferred, serials = [], iter(range(1 << 20))

        def when(token, work, *args):
            deferred.append((token[2], next(serials), work, args))

        def run_deferred(until):
            ran = False
            while deferred and min(deferred)[0] <= until:
                first = min(deferred)
                deferred.remove(first)
                first[2](*first[3])
                ran = True
            return ran

        rest_read = [None, None]
        parts_done = {}
        fill_done = {}

        def qk_unit(p, which, half):
            b, m = p // PAIRS, p % PAIRS
            w_sb = (wq_sb, wk_sb)[which]
            pe.wait(qk_weights, xT_loaded[b])
            n, bank = take_bank()
            for j in range(M):
                done = pe.do(TE.matmul, bank[:, :], w_sb[:, j, m * P:(m + 1) * P],
                             xT_sb[:, j, half * BANK:(half + 1) * BANK], start=(j == 0), stop=(j == M - 1),
                             signal=pe_dense if j == M - 1 else None)
                if j < M - 1:
                    yield
            xT_read[0] = done
            when(done, split_parts, p, which, half, n, bank, done)

        def split_parts(p, which, half, n, bank, done):
            bias = bqk_sb[:, which, p % PAIRS:p % PAIRS + 1]
            part = [parts[:, which, i, half * BANK:(half + 1) * BANK] for i in range(PARTS)]
            if p > 0:
                act.wait(*fill_done[2 * p - 2], *fill_done[2 * p - 1])
                dve.wait(*fill_done[2 * p - 2], *fill_done[2 * p - 1])
                pool.wait(*fill_done[2 * p - 2], *fill_done[2 * p - 1])
            act.wait(done)
            first = act.do(SE.activation, part[0], bank[:, :], ACT.Identity, bias=bias, scale=1.0, signal=act_dense)
            k = half
            dve.wait(done, first, rest_read[k])
            rest = dve.do(VE.scalar_tensor_tensor, out=part_rest[k][:, :], in0=bank[:, :], scalar=bias,
                          in1=part[0], op0=ALU.add, op1=ALU.subtract, signal=dve_dense)
            bank_was_read(n, rest)
            dve.wait(rest)
            second = dve.do(VE.tensor_copy, part[1], part_rest[k][:, :], signal=dve_dense)
            pool.wait(second)
            third = pool.do(GE.tensor_tensor, part[2], part_rest[k][:, :], part[1], ALU.subtract, signal=pool_dense)
            rest_read[k] = third
            parts_done.setdefault(p, []).append(third)

        exp_read = {}

        def fill(g, c):
            slot, p = g % 3, g // 2
            lane = (g % 2) * G + c
            src = parts[lane * HD:(lane + 1) * HD, :, :, :]
            sp.wait(parts_done[p][-1], exp_read.get(g - 3))
            q, k = stack_q[slot], stack_k[slot]
            for dst, a in (
                (k[0:ROWS3, c, :], src[:, 1, :, :]),
                (q[0:ROWS3, c, :], src[:, 0, 0:1, :].broadcast_to([HD, 3, T])),
                (k[ROWS3:ROWS2, c, :], src[:, 1, 0:2, :]),
                (q[ROWS3:ROWS2, c, :], src[:, 0, 1:2, :].broadcast_to([HD, 2, T])),
                (k[ROWS2:ROWS, c, :], src[:, 1, 0, :]),
                (q[ROWS2:ROWS, c, :], src[:, 0, 2, :]),
            ):
                done = sp.do(DMA.dma_start, dst, a, signal=s_fill[slot][c])
            fill_done.setdefault(g, []).append(done)

        v_done = {}

        def v_unit(b, t2):
            pe.wait(weights, xT_loaded[b])
            n, bank = take_bank()
            for i in range(2):
                for j in range(M):
                    tok = (2 * t2 + i) * P
                    done = pe.do(TE.matmul, bank[:, i * D:(i + 1) * D], xT_sb[:, j, tok:tok + P], wv_sb[:, j, :],
                                 start=(j == 0), stop=(j == M - 1), signal=pe_dense if i and j else None)
                if i == 0:
                    yield
            xT_read[0] = done
            when(done, v_store, b, t2, n, bank, done)

        def v_store(b, t2, n, bank, done):
            dve.wait(done, weights, constants, pv_done.get(b * GROUPS - 1))
            by_head = "p (r e c d) -> p r e c d"
            dims = dict(e=2, c=G, d=HD)
            bias = bv_sb[:, :].rearrange(by_head, **dims)
            for i in range(2):
                src = bank[:, i * D:(i + 1) * D].rearrange(by_head, **dims)
                dst = v_ones[:, 2 * t2 + i, :, :].rearrange("p (r e c) d -> p r e c d", e=2, c=G)
                for e in range(2):
                    t = dve.do(VE.tensor_tensor, dst[:, :, e, :, e * HD:(e + 1) * HD], src[:, :, e, :, :],
                               bias[:, :, e, :, :], ALU.add, signal=dve_dense)
            bank_was_read(n, t)
            v_done.setdefault(b, []).append(t)

        turns_due = []
        max_done, row_read, neg_sent, maxrow_done = [], [None], [None], {}

        def max_unit(g, n):
            c, u = n // UNITS, n % UNITS
            slot, bank = g % 3, max_ps[n % 2]
            pe.wait(fill_done[g][c], constants)
            if g or n >= 2:
                pe.wait(max_done[g * SLOTS + n - 2])
            for s, (i, k0, count, at) in enumerate(MAX_UNITS[u]):
                diagonal = k0 + count - 1 == i
                end = (at + count) * P
                final = s == len(MAX_UNITS[u]) - 1
                done = pe.do(TE.matmul, bank[:, at * P:end], stack_q[slot][0:ROWS, c, i * P:(i + 1) * P],
                             stack_k[slot][0:ROWS, c, k0 * P:(k0 + count) * P], start=True, stop=not diagonal,
                             signal=pe_max if final and not diagonal else None)
                if diagonal:
                    done = pe.do(TE.matmul, bank[:, end - P:end], identity_bf[:, :], causal[:, :],
                                 start=False, stop=True, signal=pe_max if final else None)
            when(done, take_max, g, n, bank, done)

        def take_max(g, n, bank, done):
            c, u = n // UNITS, n % UNITS
            first, count = PARTIAL[u]
            dve.wait(done)
            max_done.append(dve.do(VE.tensor_reduce, partial_max[:, c, first:first + count],
                                   bank[:, :].rearrange("p (a b) -> p a b", a=count), AX_X, ALU.max,
                                   signal=dve_max))
            if n == SLOTS - 1:
                max_rows(g)

        def max_rows(g):
            dve.wait(max_done[-1], row_read[0])
            for i, (first, count) in enumerate(PARTIAL_OF_BLOCK):
                done = dve.do(VE.tensor_reduce, row_max[:, :, i], partial_max[:, :, first:first + count],
                              AX_X, ALU.max, signal=dve_row)
            turns_due.append((g, done))

        def max_turn(g, done):
            pe.wait(done, constants)
            n, bank = take_bank()
            done = pe.do(TE.transpose, bank[0:G * C, 0:P], row_max[:, :, :].rearrange("p c i -> p (c i)"),
                         identity[:, :], signal=pe_dense)
            row_read[0] = done
            when(done, negate, g, n, bank, done)

        def negate(g, n, bank, done):
            rows = bank[0:G * C, 0:P]
            dve.wait(done, neg_sent[0])
            t = dve.do(VE.tensor_scalar, neg_max[:, 0, :], rows, -1.0, None, ALU.mult, signal=dve_dense)
            dve.wait(t)
            t = dve.do(VE.scalar_tensor_tensor, out=neg_rest[:, :], in0=rows, scalar=-1.0, in1=neg_max[:, 0, :],
                       op0=ALU.mult, op1=ALU.subtract, signal=dve_dense)
            bank_was_read(n, t)
            dve.wait(t)
            t = dve.do(VE.tensor_copy, neg_max[:, 1, :], neg_rest[:, :], signal=dve_dense)
            dve.wait(t)
            t = dve.do(VE.tensor_tensor, neg_max[:, 2, :], neg_rest[:, :], neg_max[:, 1, :], ALU.subtract,
                       signal=dve_dense)
            sp.wait(t, exp_read.get(g - 3))
            for i in range(PARTS):
                t = sp.do(DMA.dma_start, stack_q[g % 3][ROWS + i:ROWS + i + 1, :, :].rearrange("p c t -> p (c t)"),
                          neg_max[:, i, :], signal=s_maxrow[g % 3])
            neg_sent[0] = maxrow_done[g] = t

        exp_done, prob_done, pv_done, pv_of_set = [], [], {}, []

        def exp_unit(g, n):
            u, c = n // G, n % G
            slot, serial = g % 3, g * SLOTS + n
            bank, p_sb = exp_ps[serial % 2], prob[serial % P_RING]
            pe.wait(maxrow_done[g], ones_rows)
            if serial >= 2:
                pe.wait(exp_done[serial - 2])
            for s, (j, q0, count, at) in enumerate(EXP_UNITS[u]):
                final = s == len(EXP_UNITS[u]) - 1
                done = pe.do(TE.matmul, bank[:, at * P:(at + count) * P],
                             stack_k[slot][0:ROWS_MAX, c, j * P:(j + 1) * P],
                             stack_q[slot][0:ROWS_MAX, c, q0 * P:(q0 + count) * P], start=True, stop=True,
                             signal=pe_exp if final else None)
            if n == SLOTS - 1:
                exp_read[g] = done
            when(done, exponential, g, n, bank, p_sb, done)

        def exponential(g, n, bank, p_sb, done):
            u, serial = n // G, g * SLOTS + n
            act.wait(done)
            if serial >= P_RING:
                act.wait(pv_of_set[(serial - P_RING) // G])
            t = act.do(SE.activation, p_sb[:, :], bank[:, :], ACT.Exp, scale=SCALE, signal=act_exp)
            exp_done.append(t)
            when(t, cut_future, u, serial, p_sb, t)

        def cut_future(u, serial, p_sb, t):
            for j, q0, count, at in EXP_UNITS[u]:
                if j == q0:
                    pool.wait(exp_done[serial])
                    block = p_sb[:, at * P:(at + 1) * P]
                    t = pool.do(GE.affine_select, out=block, in_=block, compare_op=ALU.is_ge, fill=0.0, base=0,
                                pattern=[[1, P]], channel_multiplier=-1, signal=pool_mask)
            prob_done.append(t)

        o_read, o_stored = [None], [0]

        def pv_set(g, u):
            first = g * SLOTS + u * G
            b, h0 = g // GROUPS, (g % GROUPS) * G
            pe.wait(v_done[b][-1])
            if u == 0:
                pe.wait(o_read[0])
            final = u == UNITS - 1
            for s, (j, q0, count, at) in enumerate(EXP_UNITS[u]):
                for c in range(G):
                    if s == 0:
                        pe.wait(prob_done[first + c])
                    end = s == len(EXP_UNITS[u]) - 1 and c == G - 1
                    done = pe.do(TE.matmul, o_ps[32 * c:32 * c + 32, q0 * P:(q0 + count) * P],
                                 v_ones[:, j, h0 + c, :], prob[(first + c) % P_RING][:, at * P:(at + count) * P],
                                 start=(u < 2), stop=final, signal=pe_pv if end else None,
                                 ns=count * P * 4 / 2.4 / G + 20)
            pv_of_set.append(done)
            if final:
                pv_done[g] = done
                when(done, o_store, g)

        scaled_read = [None, None]
        inv_rows_read, inv_wide_read, attn_read, attn_done = [None], [None], [None], {}

        def o_store(g):
            e = g % 2
            act.wait(pv_done[g], scaled_read[e])
            t = act.do(SE.copy, o_sb[e][:, :], o_ps[:, :], signal=act_o)
            o_read[0] = t
            o_stored[0] = g + 1
            first = HD * (1 - e)
            sp.wait(t)
            for c in range(G):
                row = 32 * c + first
                t = sp.do(DMA.dma_start, sums[32 * c:32 * c + 32, :], o_sb[e][row:row + 1, :], signal=s_sums)
            when(t, invert, g, t)

        def invert(g, t):
            dve.wait(t)
            t = dve.do(VE.reciprocal, inv_sums[:, :], sums[:, :], signal=dve_dense)
            sp.wait(t, inv_rows_read[0], constants)
            for c in range(G):
                t = sp.do(DMA.dma_start, inv_rows[32 * c:32 * c + 1, :], inv_sums[32 * c:32 * c + 32, :], signal=s_inv)
            when(t, spread, g, t)

        def spread(g, t):
            e, r = g % 2, (g % GROUPS) // 2
            mask = [1] * 32
            mask[e * HD:(e + 1) * HD] = [0] * HD
            dve.wait(t, inv_wide_read[0])
            t = dve.do(VE.stream_shuffle, inv_wide[:, :], inv_rows[:, :], mask, signal=dve_dense)
            inv_rows_read[0] = t
            pool.wait(t)
            if e == 0:
                pool.wait(attn_read[0] if r == 0 else None)
                t = pool.do(GE.tensor_tensor, attn[:, r, :], o_sb[0][:, :], inv_wide[:, :], ALU.mult, signal=pool_dense)
            else:
                t = pool.do(GE.tensor_tensor, o_sb[1][:, :], o_sb[1][:, :], inv_wide[:, :], ALU.mult, signal=pool_dense)
            inv_wide_read[0] = t
            if e == 1:
                pool.wait(t)
                t = pool.do(GE.tensor_tensor, attn[:, r, :], attn[:, r, :], o_sb[1][:, :], ALU.add, signal=pool_dense)
            scaled_read[e] = t
            attn_done[g] = t

        ln_turn, ln_open, ln_used = [0], [False, False], [None, None]

        def layer_norm(bank, n, residual, outs, before, finish):
            k = ln_turn[0] % 2
            ln_turn[0] += 1
            assert not ln_open[k]
            ln_open[k] = True
            y, stats, mv = ln_in[k], ln_stats[k], ln_mv[k]
            dve.wait(ln_used[k], *before)
            t = dve.do(VE.tensor_tensor, y[:, :, :], bank[:, :].rearrange("p (i d) -> p i d", i=2), residual,
                       ALU.add, signal=dve_dense)
            bank_was_read(n, t)
            dve.wait(t)
            for i in range(2):
                t = dve.do(VE.bn_stats, stats[:, i, :], y[:, i, :], signal=dve_dense)
            dve.wait(t)
            for i in range(2):
                t = dve.do(VE.bn_aggr, mv[:, i, :], stats[:, i, :], signal=dve_dense)
            dve.wait(t)
            t = dve.do(VE.tensor_scalar, ln_var[k][:, :], mv[:, :, 1], EPS, None, ALU.add, signal=dve_dense)
            pool.wait(t, constants)
            t = pool.do(GE.tensor_tensor, ln_rstd[k][:, :], ln_var[k][:, :], minus_half[:, :], ALU.pow,
                        signal=pool_dense)
            when(t, normalise, k, outs, t, finish)

        def normalise(k, outs, t, finish):
            dve.wait(t)
            for i in range(2):
                t = dve.do(VE.tensor_scalar, outs[i], ln_in[k][:, i, :], ln_mv[k][:, i, 0:1], ln_rstd[k][:, i:i + 1],
                           ALU.subtract, ALU.mult, signal=dve_dense)
            ln_used[k], ln_open[k] = t, False
            finish(t)

        x_ready, x1_used, x1_done = {}, {}, {}

        def load_x(b):
            sp.wait(x1_used.get((b - 1, C // 2 - 1)))
            t = sp.do(DMA.dma_start, x1[:, :, :], x[b].rearrange("(c p) d -> p c d", p=P), signal=s_x)
            when(t, add_bo, b, t)

        def add_bo(b, t):
            pool.wait(t, weights)
            x_ready[b] = pool.do(GE.tensor_tensor, x1[:, :, :], x1[:, :, :],
                                 bo_sb[:, :].rearrange("p (o d) -> p o d", o=1).broadcast_to([P, C, D]),
                                 ALU.add, signal=pool_dense)

        def wo_unit(b, t2):
            pe.wait(weights, attn_done[(b + 1) * GROUPS - 1])
            n, bank = take_bank()
            for i in range(2):
                tok = (2 * t2 + i) * P
                for r in range(PAIRS):
                    done = pe.do(TE.matmul, bank[:, i * D:(i + 1) * D], attn[:, r, tok:tok + P], wo_sb[:, r, :],
                                 start=(r == 0), stop=(r == PAIRS - 1), signal=pe_dense if i and r else None)
                if i == 0:
                    yield
            attn_read[0] = done
            when(done, ln1, b, t2, n, bank, done)

        def ln1(b, t2, n, bank, done):
            rows = x1[:, 2 * t2:2 * t2 + 2, :]

            def finish(t):
                x1_done[(b, t2)] = t

            layer_norm(bank, n, rows, [rows[:, 0, :], rows[:, 1, :]], [done, x_ready[b]], finish)

        x1T_done, x1T_free, x1_turned, mean_done = {}, [None], {}, {}

        def turn_unit(b, half, m):
            pe.wait(x1_done[(b, 2 * half)], x1_done[(b, 2 * half + 1)], constants)
            n, bank = take_bank()
            for i in range(CH):
                done = pe.do(TE.transpose, bank[:, i * P:(i + 1) * P],
                             x1[:, half * CH + i, m * P:(m + 1) * P], identity[:, :],
                             signal=pe_dense if i == CH - 1 else None)
            x1_turned[b] = done
            when(done, turn_store, b, half, m, n, bank, done)
            yield

        def turn_store(b, half, m, n, bank, done):
            act.wait(done, x1T_free[0])
            t = act.do(SE.activation, x1T[:, m, half * BANK:(half + 1) * BANK], bank[:, :], ACT.Copy,
                       accum_out=x1_sum[:, m, half:half + 1], signal=act_dense)
            bank_was_read(n, t)
            x1T_done.setdefault((b, half), []).append(t)
            if half == HALVES - 1 and len(x1T_done[(b, half)]) == M:
                when(t, column_sums, b)

        w_free, w1_loaded, w2_loaded, b2_added = [None], {}, {}, {}

        def column_sums(b):
            dve.wait(x1T_done[(b, HALVES - 1)][-1])
            mean_done[b] = dve.do(VE.tensor_reduce, x1_mean[:, :], x1_sum[:, :, :], AX_X, ALU.add, signal=dve_dense)

        def route_unit(b):
            pe.wait(mean_done[b], weights)
            n, bank = take_bank()
            for m in range(M):
                done = pe.do(TE.matmul, bank[0:1, 0:E], x1_mean[:, m:m + 1], wr_sb[:, m, :], start=(m == 0),
                             stop=(m == M - 1), signal=pe_dense if m == M - 1 else None)
            when(done, pick, b, n, bank, done)
            yield

        def pick(b, n, bank, done):
            dve.wait(done, weights)
            t = dve.do(VE.scalar_tensor_tensor, out=route[:, :], in0=bank[0:1, 0:E], scalar=1.0 / T,
                       in1=br_sb[:, :], op0=ALU.mult, op1=ALU.add, signal=dve_dense)
            bank_was_read(n, t)
            dve.wait(t)
            t = dve.do(VE.max, route_top[:, :], route[:, :], signal=dve_dense)
            dve.wait(t, w2_loaded.get(b - 1))
            t = dve.do(VE.max_index, route_at[:, :], route_top[:, :], route[:, :], signal=dve_dense)
            when(t, load_expert, b, t)

        def load_expert(b, t):
            sp.wait(t, w_free[0])

            def issue(kind):
                if kind == 0:
                    expert = nc.sync.value_load(route_at[0:1, 0:1], min_val=0, max_val=E - 1)
                    issue.expert = expert
                    return nc.sync.dma_start(w1_sb[:, :, :],
                                             w1[bass.ds(expert, 1), :, :].rearrange("e (m p) f -> p (e m) f", p=P))
                if kind == 1:
                    return nc.sync.dma_start(b1_sb[:, :],
                                             b1T[bass.ds(issue.expert, 1), :, :].rearrange("e p f -> p (e f)"))
                if kind == 2:
                    return nc.sync.dma_start(w2_sb[:, :, :],
                                             w2[bass.ds(issue.expert, 1), :, :].rearrange("e (m p) d -> p (e m) d", p=P))
                return nc.sync.dma_start(b2_sb[:, :], b2[bass.ds(issue.expert, 1), :].broadcast_to([P, D]))

            for kind, signal in ((0, s_w1), (1, s_w1), (2, s_w2), (3, s_w2)):
                t = sp.do(issue, kind, signal=signal)
                (w1_loaded if kind < 2 else w2_loaded)[b] = t
            when(t, add_b2, b)

        def add_b2(b):
            pool.wait(w2_loaded[b], x1_turned[b])
            b2_added[b] = pool.do(GE.tensor_tensor, x1[:, :, :], x1[:, :, :],
                                  b2_sb[:, :].rearrange("p (o d) -> p o d", o=1).broadcast_to([P, C, D]),
                                  ALU.add, signal=pool_dense)

        hidden_done, hidden_free = {}, [None]

        def ffn1_unit(b, half, f):
            pe.wait(w1_loaded[b], x1T_done[(b, half)][-1])
            n, bank = take_bank()
            for m in range(M):
                done = pe.do(TE.matmul, bank[:, :], w1_sb[:, m, f * P:(f + 1) * P],
                             x1T[:, m, half * BANK:(half + 1) * BANK], start=(m == 0), stop=(m == M - 1),
                             signal=pe_dense if m == M - 1 else None)
                if m < M - 1:
                    yield
            if f == FC - 1 and half == HALVES - 1:
                x1T_free[0] = done
            when(done, relu, b, half, f, n, bank, done)

        def relu(b, half, f, n, bank, done):
            act.wait(done, hidden_free[0])
            t = act.do(SE.activation, hidden[:, f, :], bank[:, :], ACT.Relu, bias=b1_sb[:, f:f + 1], scale=1.0,
                       signal=act_dense)
            bank_was_read(n, t)
            hidden_done.setdefault((b, half), []).append(t)

        def ffn2_unit(b, half, t2):
            pe.wait(w2_loaded[b], hidden_done[(b, half)][-1])
            n, bank = take_bank()
            for i in range(2):
                tok = (2 * t2 + i) * P
                for f in range(FC):
                    done = pe.do(TE.matmul, bank[:, i * D:(i + 1) * D], hidden[:, f, tok:tok + P], w2_sb[:, f, :],
                                 start=(f == 0), stop=(f == FC - 1),
                                 signal=pe_dense if i and f == FC - 1 else None)
                    if f % 2 and not (i and f == FC - 1):
                        yield
            if t2 == CH // 2 - 1:
                hidden_free[0] = done
                if half == HALVES - 1:
                    w_free[0] = done
            when(done, ln2, b, half, t2, n, bank, done)

        y_sent = [None, None]

        def ln2(b, half, t2, n, bank, done):
            blocks = half * CH + 2 * t2
            k = (blocks // 2) % 2
            y = y_out[k]

            def finish(t):
                rows = out[b].rearrange("(c p) d -> p c d", p=P)
                sp.wait(t)
                y_sent[k] = sp.do(DMA.dma_start, rows[:, blocks:blocks + 2, :], y[:, :, :], signal=s_out[k])

            layer_norm(bank, n, x1[:, blocks:blocks + 2, :], [y[:, 0, :], y[:, 1, :]],
                       [done, b2_added[b], y_sent[k]], finish)
            x1_used[(b, blocks // 2)] = bank_read[n]

        def parts_ready(p):
            return len(parts_done.get(p, ())) == 2 * HALVES

        def prep_stream():
            for b in range(B):
                for r in range(PAIRS):
                    p = b * PAIRS + r
                    start = (2 * p - 3) * SLOTS + 6
                    if r == 1:
                        for t2 in range(C // 2):
                            yield (b * GROUPS * SLOTS + t2, lambda b=b: b == 0 or b * GROUPS - 1 in pv_done,
                                   v_unit(b, t2))
                    for i in range(2 * HALVES):
                        yield (start + 4 * i,
                               lambda b=b, p=p: xT_loaded[b] and (p == 0 or len(fill_done.get(2 * p - 1, ())) == G),
                               qk_unit(p, i % 2, i // 2))

        def post_stream():
            for b in range(B):
                at, span = ((b + 1) * GROUPS) * SLOTS + 8, GROUPS * SLOTS - 8
                units = [(lambda b=b: (b + 1) * GROUPS - 1 in attn_done and b in x_ready, wo_unit(b, t2), 1)
                         for t2 in range(C // 2)]
                for half in range(HALVES):
                    units += [(lambda b=b, t=2 * half + 1: (b, t) in x1_done, turn_unit(b, half, m), .3)
                              for m in range(M)]
                units += [(lambda b=b: b in mean_done, route_unit(b), .2)]
                for half in range(HALVES):
                    units += [(lambda b=b, half=half: b in w2_loaded and
                               (half == 0 or len(hidden_done.get((b, 0), ())) == FC and hidden_free[0] is not None),
                               ffn1_unit(b, half, f), 1) for f in range(FC)]
                    units += [(lambda b=b, half=half: len(hidden_done.get((b, half), ())) == FC and b in b2_added,
                               ffn2_unit(b, half, t2), 4) for t2 in range(CH // 2)]
                total, done = sum(u[2] for u in units), 0
                for ready, unit, weight in units:
                    yield (at + span * done / total, ready, unit)
                    done += weight

        streams = [list(prep_stream()), list(post_stream())]
        exps = maxes = sets = 0
        dense_unit = None
        fills, next_x, next_xT = 0, 0, 1

        def started(*tokens):
            return max([pe.clock] + [t[2] for t in tokens if t])

        while True:
            run_deferred(pe.clock)
            if fills < LAST * G and sp.clock < pe.clock + 2000:
                g, c = fills // G, fills % G
                if parts_ready(g // 2) and (g < 3 or g - 3 in exp_read):
                    fill(g, c)
                    fills += 1
            if next_xT < B and not dense_unit and streams[0] and streams[0][0][0] >= (2 * next_xT * PAIRS - 3) * SLOTS:
                xT_loaded[next_xT] = load_xT(next_xT)
                next_xT += 1
            if next_x < B and (next_x == 0 or (next_x - 1, C // 2 - 1) in x1_used):
                load_x(next_x)
                next_x += 1

            choices = []
            if exps < LAST * SLOTS:
                g = exps // SLOTS
                if g in maxrow_done and len(exp_done) > exps - 2 and (
                        exps < P_RING or len(pv_of_set) > (exps - P_RING) // G):
                    choices.append((exps, started(maxrow_done[g], exp_done[exps - 2] if exps > 1 else None), "exp"))
            if maxes < LAST * SLOTS:
                g, n = maxes // SLOTS, maxes % SLOTS
                if len(fill_done.get(g, ())) > n // UNITS and len(max_done) > maxes - 2 and (g < 1 or g - 1 in maxrow_done):
                    choices.append(((g - 1) * SLOTS + n * MAX_SLOTS / SLOTS,
                                    started(fill_done[g][n // UNITS], max_done[maxes - 2] if maxes > 1 else None), "max"))
            if sets < LAST * UNITS:
                g, u = sets // UNITS, sets % UNITS
                if len(prob_done) >= G * (sets + 1) and len(v_done.get(g // GROUPS, ())) == C // 2 and (
                        u or g == 0 or o_stored[0] == g):
                    choices.append((G * sets + G, started(prob_done[G * sets + G - 1], o_read[0], v_done[g // GROUPS][-1]), "pv"))
            if dense_unit:
                choices.append((dense_unit[0], pe.clock, "go on"))
            elif bank_ready():
                free = started(bank_read[banks_taken[0] % 2])
                if turns_due:
                    choices.append((-1, max(free, turns_due[0][1][2]), "turn"))
                for i, stream in enumerate(streams):
                    if stream and stream[0][1]():
                        choices.append((stream[0][0], free, i))
            if not choices:
                if not deferred:
                    break
                pe.clock = max(pe.clock, min(deferred)[0])
                continue
            near = [c for c in choices if c[1] <= pe.clock + NEAR]
            turn, at, what = min(near, key=lambda c: c[0]) if near else min(choices, key=lambda c: c[1])
            if not near and deferred and min(deferred)[0] < at:
                pe.clock = max(pe.clock, min(deferred)[0])
                continue
            if what == "exp":
                exp_unit(exps // SLOTS, exps % SLOTS)
                exps += 1
            elif what == "max":
                max_unit(maxes // SLOTS, maxes % SLOTS)
                maxes += 1
            elif what == "pv":
                pv_set(sets // UNITS, sets % UNITS)
                sets += 1
            elif what == "turn":
                max_turn(*turns_due.pop(0))
            else:
                if what != "go on":
                    dense_unit = streams[what].pop(0)
                if next(dense_unit[2], "end") == "end":
                    dense_unit = None
        assert exps == maxes == LAST * SLOTS and sets == LAST * UNITS and not any(streams)
        sp.wait(*y_sent)

        block = ctx.enter_context(nc.Block())

        @block.tensor
        def _(engine):
            pe.play(engine)

        @block.vector
        def _(engine):
            dve.play(engine)

        @block.scalar
        def _(engine):
            act.play(engine)

        @block.gpsimd
        def _(engine):
            pool.play(engine)

        @block.sync
        def _(engine):
            sp.play(engine)


def kernel(L0_attn_x, L0_attn_wq, L0_attn_bq, L0_attn_wk, L0_attn_bk, L0_attn_wv, L0_attn_bv, L0_attn_wo,
           L0_attn_bo, L0_ffn_Wr, L0_ffn_br, L0_ffn_W1, L0_ffn_b1, L0_ffn_W2, L0_ffn_b2):
    import numpy as np
    import concourse.bacc as bacc
    from concourse.bass_utils import run_bass_kernel_spmd

    x = np.asarray(L0_attn_x)
    D = x.shape[-1]
    E = L0_ffn_W1.shape[0]
    wo = np.asarray(L0_attn_wo).reshape(D // P, 2, G, HD, D).transpose(0, 2, 1, 3, 4).reshape(D, D)
    bqkT = np.stack([np.asarray(L0_attn_bq).reshape(-1, P).T, np.asarray(L0_attn_bk).reshape(-1, P).T], axis=1)
    layouts = {
        "x": x, "xT": x.transpose(0, 2, 1),
        "wq": L0_attn_wq, "wk": L0_attn_wk, "wv": L0_attn_wv, "bqkT": bqkT,
        "bv": np.asarray(L0_attn_bv).reshape(1, -1), "wo": wo, "bo": np.asarray(L0_attn_bo).reshape(1, -1),
        "wr": L0_ffn_Wr, "br": np.asarray(L0_ffn_br).reshape(1, -1),
        "w1": L0_ffn_W1, "b1T": np.asarray(L0_ffn_b1).reshape(E, -1, P).transpose(0, 2, 1),
        "w2": L0_ffn_W2, "b2": L0_ffn_b2,
    }
    nc = bacc.Bacc("TRN2", target_bir_lowering=False, num_devices=1)
    arrays, args = {}, []
    for name, a in layouts.items():
        a = np.ascontiguousarray(a)
        arrays[f"in_{name}"] = a
        args.append(nc.dram_tensor(f"in_{name}", a.shape, mybir.dt.from_np(a.dtype), kind="ExternalInput").ap())
    out = nc.dram_tensor("out", x.shape, mybir.dt.from_np(x.dtype), kind="ExternalOutput").ap()
    post_ln_layer(nc, *args, out)
    r = run_bass_kernel_spmd(nc, [arrays], core_ids=[0])
    return r.results[0]["out"]
```

```python
from contextlib import ExitStack

import concourse.bass as bass
from concourse import mybir

F32 = mybir.dt.float32
F32R = mybir.dt.float32r
BF16 = mybir.dt.bfloat16
U32 = mybir.dt.uint32
ALU = mybir.AluOpType
ACT = mybir.ActivationFunctionType
AX_X = mybir.AxisListType.X

P = 128
HD = 16
G = 4
BANK = 512
PARTS = 3
EPS = 1e-5
MASKED = -3.0e38
DMA_DONE = 16

ROWS3 = 3 * HD
ROWS2 = ROWS3 + 2 * HD
ROWS = ROWS2 + HD

EXP_UNITS = [
    [(0, 0, 4, 0)], [(0, 4, 4, 0)], [(1, 4, 4, 0)], [(2, 4, 4, 0)], [(3, 4, 4, 0)], [(4, 4, 4, 0)],
    [(1, 1, 3, 0), (7, 7, 1, 3)], [(3, 3, 1, 0), (5, 5, 3, 1)], [(2, 2, 2, 0), (6, 6, 2, 2)],
]
MAX_UNITS = [
    [(4, 0, 4, 0)], [(5, 0, 4, 0)], [(6, 0, 4, 0)], [(7, 0, 4, 0)], [(3, 0, 4, 0)], [(7, 4, 4, 0)],
    [(2, 0, 3, 0), (4, 4, 1, 3)], [(0, 0, 1, 0), (6, 4, 3, 1)], [(1, 0, 2, 0), (5, 4, 2, 2)],
]
UNITS = len(EXP_UNITS)
PARTIAL_OF_BLOCK, TAKES, PARTIALS = [], [[] for _ in MAX_UNITS], 0
for block in range(8):
    first = PARTIALS
    for u, segments in enumerate(MAX_UNITS):
        for i, k0, count, at in segments:
            if i == block:
                TAKES[u].append((at, count, k0 + count - 1 == i, PARTIALS))
                PARTIALS += 1
    PARTIAL_OF_BLOCK.append((first, PARTIALS - first))
SLOTS = UNITS * G
MAX_SLOTS = 26
MAX_LEAD = 10
V_LEAD = 4
QK_AT = 34
QK_EVERY = 4
POST_AT = 36
POST_END = 20
PV_AT = 2
TAIL = 30
DVE_SPARE = 2500
OPEN_AT = 16e3
X_AT = 60e3
NEAR = 90


class Signal:

    def __init__(self, sem, by=1):
        self.sem, self.by, self.count = sem, by, 0

    def mark(self, at):
        self.count += self.by
        return (self, self.count, at)


class Queue:

    def __init__(self, price, latency):
        self.ops, self.waited, self.clock, self.price, self.latency = [], {}, 0.0, price, latency

    def wait(self, *tokens):
        for token in tokens:
            if token is None:
                continue
            signal, value, at = token
            self.clock = max(self.clock, at)
            if self.waited.get(signal, 0) < value:
                self.waited[signal] = value
                self.ops.append((None, signal.sem, value, None, None))

    def do(self, method, *args, signal=None, ns=None, **kw):
        self.ops.append((method, args, kw, signal and signal.sem, signal and signal.by))
        self.clock += self.price(args, kw) if ns is None else ns
        return signal.mark(self.clock + self.latency) if signal else None

    def play(self, engine):
        for method, a, b, sem, by in self.ops:
            if method is None:
                engine.wait_ge(a, b)
            else:
                made = method(*a, **b)
                if sem is not None:
                    made.then_inc(sem, by)


class TensorQueue(Queue):

    TICK, BUSY = 10240 / 3, 3060

    def __init__(self, *args):
        super().__init__(*args)
        self.tick, self.count, self.full = 0, 0.0, False

    def do(self, method, *args, ns=None, **kw):
        tick = self.clock // self.TICK
        if tick > self.tick:
            self.full = tick == self.tick + 1 and self.count >= self.BUSY
            self.tick, self.count = tick, 0.0
        ns = self.price(args, kw) if ns is None else ns
        self.count += ns * 2.4 * args[1].shape[0] / P
        return super().do(method, *args, ns=ns if self.full else 2 * ns, **kw)


def columns(args, kw):
    found = [a for a in (*args[:2], kw.get("out"), kw.get("in_"), kw.get("in0")) if isinstance(a, bass.AP)]
    return max(a.free_size() for a in found)


def pe_price(args, kw):
    moving = args[2]
    passes = 4 if moving.dtype == F32 and args[0].free_size() > P else 1
    return passes * (moving.free_size() / 2.4 + 3)


def act_price(args, kw):
    return 60 + columns(args, kw) / 1.2 + (93 if "bias" in kw else 0)


def dve_price(args, kw):
    return 66 + columns(args, kw) / 0.96


def pool_price(args, kw):
    return 90 + columns(args, kw) * (1.2 if "pattern" in kw else 2.2)


def dma_price(args, kw):
    return 655


def post_ln_layer(nc, x, xT, wq, wk, wv, bqkT, bv, wo, bo, wr, br, w1, b1T, w2, b2, out):
    B, T, D = x.shape
    E, _, F = w1.shape
    C = T // P
    M = D // P
    FC = F // P
    H = D // HD
    GROUPS = H // G
    PAIRS = GROUPS // 2
    HALVES = T // BANK
    CH = BANK // P
    LAST = B * GROUPS
    P_RING = 8
    STAGE_RING = 2
    LN_RING = 2
    CHUNKS = M * F // BANK
    QT = BANK // 2
    SCALE = 1.0 / float(HD) ** 0.5

    with ExitStack() as ctx:
        def sb(name, shape, dt=F32):
            return ctx.enter_context(nc.sbuf_tensor(name, shape, dt))

        def ps(name, cols=BANK):
            return ctx.enter_context(nc.psum_tensor(name, [P, cols], F32))

        def sig(name, by=1):
            return Signal(ctx.enter_context(nc.semaphore(name)), by)

        identity = sb("identity", [P, P])
        causal = sb("causal", [P, BANK], BF16)
        ones = sb("ones", [P, 1])
        wq_sb, wk_sb, wv_sb = (sb(n, [P, M, D]) for n in ("wq_sb", "wk_sb", "wv_sb"))
        wo_sb = sb("wo_sb", [P, PAIRS, D])
        wr_sb = sb("wr_sb", [P, M, E])
        bqk_sb = sb("bqk_sb", [P, 2, M])
        bv_sb, bo_sb, b2_sb = (sb(n, [P, D]) for n in ("bv_sb", "bo_sb", "b2_sb"))
        br_sb = sb("br_sb", [1, E])
        b1_sb = sb("b1_sb", [P, FC])
        xT_sb = sb("xT_sb", [P, M, T])
        parts = sb("parts", [P, 2, PARTS, T], BF16)
        part_rest = sb("part_rest", [P, BANK])
        stack_q = [sb(f"stack_q{i}", [P, G, T], BF16) for i in range(3)]
        stack_k = [sb(f"stack_k{i}", [P, G, T], BF16) for i in range(3)]
        v_ones = sb("v_ones", [P, C, H, 2 * HD])
        partial_max = sb("partial_max", [P, G, PARTIALS])
        row_max = sb("row_max", [P, G, C])
        neg_max = sb("neg_max", [G * C, PARTS, P], BF16)
        neg_rest = sb("neg_rest", [G * C, P])
        prob = [sb(f"prob{i}", [P, BANK]) for i in range(P_RING)]
        o_sb = sb("o_sb", [P, T])
        sums = sb("sums", [P, G * T // P])
        inv_rows = sb("inv_rows", [P, T])
        inv_wide = sb("inv_wide", [P, BANK])
        attn = sb("attn", [P, PAIRS, T])
        x1_sb = sb("x1_sb", [P, C, D])
        x1T_hi, x1T_lo = (sb(n, [P, M, BANK], F32R) for n in ("x1T_hi", "x1T_lo"))
        x1_sum = sb("x1_sum", [P, D])
        x1_mean = sb("x1_mean", [P, M])
        route = sb("route", [1, E])
        route_top = sb("route_top", [1, 8])
        route_at = sb("route_at", [1, 8], U32)
        stage = [sb(f"stage{i}", [P, BANK]) for i in range(STAGE_RING)]
        w1_hi, w1_lo = (sb(n, [P, M, F], F32R) for n in ("w1_hi", "w1_lo"))
        w2_hi, w2_lo = (sb(n, [P, FC, D], F32R) for n in ("w2_hi", "w2_lo"))
        hidden_hi, hidden_lo = (sb(n, [P, FC, QT], F32R) for n in ("hidden_hi", "hidden_lo"))
        ln_in = [sb(f"ln_in{i}", [P, 2, D]) for i in range(LN_RING)]
        ln_stats = [sb(f"ln_stats{i}", [P, 2, 6]) for i in range(LN_RING)]
        ln_mv = [sb(f"ln_mv{i}", [P, 2, 2]) for i in range(LN_RING)]
        ln_var = [sb(f"ln_var{i}", [P, 2]) for i in range(LN_RING)]
        ln_rstd = [sb(f"ln_rstd{i}", [P, 2]) for i in range(LN_RING)]
        minus_half = sb("minus_half", [P, 2])

        max_ps = [ps(f"max_ps{i}") for i in range(2)]
        exp_ps = [ps(f"exp_ps{i}") for i in range(2)]
        dense_ps = [ps(f"dense_ps{i}") for i in range(2)]
        o_ps = ps("o_ps", T)

        s_ones = sig("s_ones")
        s_const = sig("s_const")
        s_qk = sig("s_qk", DMA_DONE)
        s_load = sig("s_load", DMA_DONE)
        s_xT = sig("s_xT", DMA_DONE)
        s_x = [sig("s_x", DMA_DONE)] * (B - 1) + [sig("s_x_last", DMA_DONE)]
        s_bias = sig("s_bias", DMA_DONE)
        s_stage = [sig(f"s_stage{i}", DMA_DONE) for i in range(STAGE_RING + P_RING)]
        s_fill = [[sig(f"s_fill{i}_{c}", DMA_DONE) for c in range(G)] for i in range(3)]
        s_maxrow = [sig(f"s_maxrow{i}", DMA_DONE) for i in range(3)]
        s_sums, s_inv = sig("s_sums", DMA_DONE), sig("s_inv", DMA_DONE)
        s_out = [sig(f"s_out{i}", DMA_DONE) for i in range(LN_RING)]
        pe_max, pe_exp, pe_pv, pe_dense = sig("pe_max"), sig("pe_exp"), sig("pe_pv"), sig("pe_dense")
        dve_max, dve_row, dve_dense = sig("dve_max"), sig("dve_row"), sig("dve_dense")
        act_exp, act_o, act_dense = sig("act_exp"), sig("act_o"), sig("act_dense")
        pool_mask, pool_dense = sig("pool_mask"), sig("pool_dense")

        pe, act, dve = TensorQueue(pe_price, 230), Queue(act_price, 70), Queue(dve_price, 70)
        pool, sp = Queue(pool_price, 100), Queue(dma_price, 2100)
        TE, VE, SE, GE, DMA = nc.tensor, nc.vector, nc.scalar, nc.gpsimd, nc.sync

        one = pool.do(GE.memset, identity[:, :], 0.0, signal=s_const)
        pool.do(GE.memset, causal[:, :], 0.0, signal=s_const)
        pool.do(GE.memset, inv_rows[:, :], 0.0, signal=s_const)
        pool.do(GE.memset, minus_half[:, :], -0.5, signal=s_const)
        zeroed = pool.do(GE.memset, v_ones[:, :, :, :], 1.0, signal=s_const)
        pool.wait(zeroed)
        t = pool.do(GE.affine_select, out=identity[:, :], in_=identity[:, :], compare_op=ALU.not_equal,
                    fill=1.0, base=0, pattern=[[-1, P]], channel_multiplier=1, signal=s_const)
        pool.do(GE.affine_select, out=causal[:, BANK - P:], in_=causal[:, BANK - P:], compare_op=ALU.is_ge,
                fill=MASKED, base=0, pattern=[[-1, P]], channel_multiplier=1, signal=s_const)
        constants = pool.do(GE.memset, ones[:, :], 1.0, signal=s_const)

        def open_rows(i):
            rows_open[i] = (dve.do(VE.memset, stack_k[i][:, :, :], 1.0, signal=s_ones, ns=4270) if i == 0 else
                            pool.do(GE.memset, stack_k[i][:, :, :], 1.0, signal=s_const, ns=3400),
                            pool.do(GE.memset, stack_q[i][:, :, :], 0.0, signal=s_const, ns=3400))

        rows_open = [None] * 3
        open_rows(0)

        def load(dst, src):
            return sp.do(DMA.dma_start, dst, src, signal=s_load)

        def load_xT(b):
            sp.wait(xT_read[0])
            return sp.do(DMA.dma_start, xT_sb[:, :, :], xT[b].rearrange("(m p) t -> p m t", p=P), signal=s_xT, ns=3000)

        xT_read = [None]
        xT_loaded = [None] * B
        xT_loaded[0] = load_xT(0)
        for dst, src in ((wq_sb, wq), (wk_sb, wk)):
            sp.do(DMA.dma_start, dst[:, :, :], src.rearrange("(m p) n -> p m n", p=P), signal=s_qk)
        qk_weights = sp.do(DMA.dma_start, bqk_sb[:, :, :], bqkT, signal=s_qk)
        load(wv_sb[:, :, :], wv.rearrange("(m p) n -> p m n", p=P))
        load(bv_sb[:, :], bv.partition_broadcast(P))
        load(wo_sb[:, :, :], wo.rearrange("(m p) n -> p m n", p=P))
        load(bo_sb[:, :], bo.partition_broadcast(P))
        load(wr_sb[:, :, :], wr.rearrange("(m p) n -> p m n", p=P))
        weights = load(br_sb[:, :], br)

        bank_read = [None, None]
        bank_open = [False, False]
        banks_taken = [0]

        def bank_ready():
            return not bank_open[banks_taken[0] % 2]

        def take_bank():
            n = banks_taken[0] % 2
            banks_taken[0] += 1
            assert not bank_open[n]
            pe.wait(bank_read[n])
            bank_open[n] = True
            return n, dense_ps[n]

        def bank_was_read(n, token):
            bank_read[n], bank_open[n] = token, False

        deferred, serials = [], iter(range(1 << 20))

        def when(token, work, *args):
            deferred.append((token[2], next(serials), work, args))

        def run_deferred(until):
            ran = False
            while deferred and min(deferred)[0] <= until:
                first = min(deferred)
                deferred.remove(first)
                first[2](*first[3])
                ran = True
            return ran

        def combine(out, a, b, op, *before):
            spare = DVE_SPARE if 0 < maxes < LAST * SLOTS else 0
            ready = max(t[2] for t in before if t)
            if max(dve.clock, ready) + spare < max(pool.clock, ready) + out.free_size():
                dve.wait(*before)
                return dve.do(VE.tensor_tensor, out, a, b, op, signal=dve_dense)
            pool.wait(*before)
            return pool.do(GE.tensor_tensor, out, a, b, op, signal=pool_dense)

        rest_read = [None]
        parts_done = {}
        fill_done = {}

        def qk_unit(p, which, half):
            b, m = p // PAIRS, p % PAIRS
            w_sb = (wq_sb, wk_sb)[which]
            pe.wait(qk_weights, xT_loaded[b])
            n, bank = take_bank()
            for i in range(2):
                tok = slice(half * BANK + i * QT, half * BANK + (i + 1) * QT)
                for j in range(M):
                    done = pe.do(TE.matmul, bank[:, i * QT:(i + 1) * QT], w_sb[:, j, m * P:(m + 1) * P],
                                 xT_sb[:, j, tok], start=(j == 0), stop=(j == M - 1),
                                 signal=pe_dense if i and j == M - 1 else None)
                    if not (i and j == M - 1):
                        yield
            xT_read[0] = done
            when(done, split_parts, p, which, half, n, bank, done)

        def split_parts(p, which, half, n, bank, done):
            bias = bqk_sb[:, which, p % PAIRS:p % PAIRS + 1]
            part = [parts[:, which, i, half * BANK:(half + 1) * BANK] for i in range(PARTS)]
            if p > 0:
                act.wait(*fill_done[2 * p - 2], *fill_done[2 * p - 1])
                dve.wait(*fill_done[2 * p - 2], *fill_done[2 * p - 1])
                pool.wait(*fill_done[2 * p - 2], *fill_done[2 * p - 1])
            act.wait(done)
            first = act.do(SE.activation, part[0], bank[:, :], ACT.Identity, bias=bias, scale=1.0, signal=act_dense)
            dve.wait(done, first, rest_read[0])
            rest = dve.do(VE.scalar_tensor_tensor, out=part_rest[:, :], in0=bank[:, :], scalar=bias,
                          in1=part[0], op0=ALU.add, op1=ALU.subtract, signal=dve_dense)
            bank_was_read(n, rest)
            dve.wait(rest)
            second = dve.do(VE.tensor_copy, part[1], part_rest[:, :], signal=dve_dense)
            third = combine(part[2], part_rest[:, :], part[1], ALU.subtract, second)
            rest_read[0] = third
            parts_done.setdefault(p, []).append(third)

        exp_read = {}

        def fill(g, c):
            slot, p = g % 3, g // 2
            lane = (g % 2) * G + c
            src = parts[lane * HD:(lane + 1) * HD, :, :, :]
            sp.wait(*parts_done[p], exp_read.get(g - 3), *rows_open[slot])
            q, k = stack_q[slot], stack_k[slot]
            for dst, a in (
                (k[0:ROWS3, c, :], src[:, 1, :, :]),
                (q[0:ROWS3, c, :], src[:, 0, 0:1, :].broadcast_to([HD, 3, T])),
                (k[ROWS3:ROWS2, c, :], src[:, 1, 0:2, :]),
                (q[ROWS3:ROWS2, c, :], src[:, 0, 1:2, :].broadcast_to([HD, 2, T])),
                (k[ROWS2:ROWS, c, :], src[:, 1, 0, :]),
                (q[ROWS2:ROWS, c, :], src[:, 0, 2, :]),
            ):
                done = sp.do(DMA.dma_start, dst, a, signal=s_fill[slot][c])
            fill_done.setdefault(g, []).append(done)

        v_done = {}

        def v_unit(b, t2):
            pe.wait(weights, xT_loaded[b])
            n, bank = take_bank()
            for i in range(2):
                for j in range(M):
                    tok = (2 * t2 + i) * P
                    done = pe.do(TE.matmul, bank[:, i * D:(i + 1) * D], xT_sb[:, j, tok:tok + P], wv_sb[:, j, :],
                                 start=(j == 0), stop=(j == M - 1), signal=pe_dense if i and j else None)
                    if not (i and j):
                        yield
            xT_read[0] = done
            when(done, v_store, b, t2, n, bank, done)

        def v_store(b, t2, n, bank, done):
            dve.wait(done, weights, constants, pv_done.get(b * GROUPS - 1))
            by_head = "p (r e c d) -> p r e c d"
            dims = dict(e=2, c=G, d=HD)
            bias = bv_sb[:, :].rearrange(by_head, **dims)
            for i in range(2):
                src = bank[:, i * D:(i + 1) * D].rearrange(by_head, **dims)
                dst = v_ones[:, 2 * t2 + i, :, :].rearrange("p (r e c) d -> p r e c d", e=2, c=G)
                for e in range(2):
                    t = dve.do(VE.tensor_tensor, dst[:, :, e, :, e * HD:(e + 1) * HD], src[:, :, e, :, :],
                               bias[:, :, e, :, :], ALU.add, signal=dve_dense)
            bank_was_read(n, t)
            v_done.setdefault(b, []).append(t)

        turns_due = []
        max_done, row_read, neg_sent, maxrow_done = [], [None], [None], {}

        def max_unit(g, n):
            c, u = n // UNITS, n % UNITS
            slot, bank = g % 3, max_ps[n % 2]
            pe.wait(fill_done[g][c])
            if g or n >= 2:
                pe.wait(max_done[g * SLOTS + n - 2])
            for s, (i, k0, count, at) in enumerate(MAX_UNITS[u]):
                final = s == len(MAX_UNITS[u]) - 1
                done = pe.do(TE.matmul, bank[:, at * P:(at + count) * P], stack_q[slot][0:ROWS, c, i * P:(i + 1) * P],
                             stack_k[slot][0:ROWS, c, k0 * P:(k0 + count) * P], start=True, stop=True,
                             signal=pe_max if final else None)
            when(done, take_max, g, n, bank, done)

        def take_max(g, n, bank, done):
            c, u = n // UNITS, n % UNITS
            dve.wait(done, constants)
            for at, count, diagonal, column in TAKES[u]:
                src, dst = bank[:, at * P:(at + count) * P], partial_max[:, c, column:column + 1]
                if diagonal:
                    t = dve.do(VE.tensor_tensor_reduce, src, src, causal[:, BANK - count * P:], 1.0, MASKED,
                               ALU.add, ALU.max, dst, signal=dve_max)
                else:
                    t = dve.do(VE.tensor_reduce, dst, src, AX_X, ALU.max, signal=dve_max)
            max_done.append(t)
            if n == SLOTS - 1:
                max_rows(g)

        def max_rows(g):
            dve.wait(max_done[-1], row_read[0])
            for i, (first, count) in enumerate(PARTIAL_OF_BLOCK):
                done = dve.do(VE.tensor_reduce, row_max[:, :, i], partial_max[:, :, first:first + count],
                              AX_X, ALU.max, signal=dve_row)
            turns_due.append((g, done))

        def max_turn(g, done):
            pe.wait(done, constants)
            n, bank = take_bank()
            done = pe.do(TE.transpose, bank[0:G * C, 0:P], row_max[:, :, :].rearrange("p c i -> p (c i)"),
                         identity[:, :], signal=pe_dense)
            row_read[0] = done
            when(done, negate, g, n, bank, done)

        def negate(g, n, bank, done):
            rows = bank[0:G * C, 0:P]
            dve.wait(done, neg_sent[0])
            t = dve.do(VE.tensor_scalar, neg_max[:, 0, :], rows, -1.0, None, ALU.mult, signal=dve_dense)
            dve.wait(t)
            t = dve.do(VE.scalar_tensor_tensor, out=neg_rest[:, :], in0=rows, scalar=-1.0, in1=neg_max[:, 0, :],
                       op0=ALU.mult, op1=ALU.subtract, signal=dve_dense)
            bank_was_read(n, t)
            dve.wait(t)
            t = dve.do(VE.tensor_copy, neg_max[:, 1, :], neg_rest[:, :], signal=dve_dense)
            dve.wait(t)
            t = dve.do(VE.tensor_tensor, neg_max[:, 2, :], neg_rest[:, :], neg_max[:, 1, :], ALU.subtract,
                       signal=dve_dense)
            sp.wait(t, exp_read.get(g - 3))
            for i in range(PARTS):
                t = sp.do(DMA.dma_start, stack_q[g % 3][ROWS + i:ROWS + i + 1, :, :].rearrange("p c t -> p (c t)"),
                          neg_max[:, i, :], signal=s_maxrow[g % 3])
            neg_sent[0] = maxrow_done[g] = t

        exp_done, prob_done, pv_done, pv_of_set = [], [], {}, []

        def exp_unit(g, n):
            u, c = n // G, n % G
            slot, serial = g % 3, g * SLOTS + n
            bank, p_sb = exp_ps[serial % 2], prob[serial % P_RING]
            pe.wait(maxrow_done[g])
            if serial >= 2:
                pe.wait(exp_done[serial - 2])
            for s, (j, q0, count, at) in enumerate(EXP_UNITS[u]):
                final = s == len(EXP_UNITS[u]) - 1
                done = pe.do(TE.matmul, bank[:, at * P:(at + count) * P],
                             stack_k[slot][:, c, j * P:(j + 1) * P],
                             stack_q[slot][:, c, q0 * P:(q0 + count) * P], start=True, stop=True,
                             signal=pe_exp if final else None)
            if n == SLOTS - 1:
                exp_read[g] = done
            when(done, exponential, g, n, bank, p_sb, done)

        def exponential(g, n, bank, p_sb, done):
            u, serial = n // G, g * SLOTS + n
            act.wait(done)
            if serial >= P_RING:
                act.wait(pv_of_set[(serial - P_RING) // G])
            t = act.do(SE.activation, p_sb[:, :], bank[:, :], ACT.Exp, scale=SCALE, signal=act_exp)
            exp_done.append(t)
            when(t, cut_future, u, serial, p_sb, t)

        def cut_future(u, serial, p_sb, t):
            for j, q0, count, at in EXP_UNITS[u]:
                if j == q0:
                    pool.wait(exp_done[serial])
                    block = p_sb[:, at * P:(at + 1) * P]
                    t = pool.do(GE.affine_select, out=block, in_=block, compare_op=ALU.is_ge, fill=0.0, base=0,
                                pattern=[[1, P]], channel_multiplier=-1, signal=pool_mask)
            prob_done.append(t)

        o_read, o_stored = [None], [0]

        def v_needed(u):
            return max(j for j, *_ in EXP_UNITS[u]) // 2


        def pv_set(g, u):
            first = g * SLOTS + u * G
            b, h0 = g // GROUPS, (g % GROUPS) * G
            pe.wait(v_done[b][v_needed(u)])
            if u == 0:
                pe.wait(o_read[0])
            final = u == UNITS - 1
            for s, (j, q0, count, at) in enumerate(EXP_UNITS[u]):
                for c in range(G):
                    if s == 0:
                        pe.wait(prob_done[first + c])
                    end = s == len(EXP_UNITS[u]) - 1 and c == G - 1
                    done = pe.do(TE.matmul, o_ps[32 * c:32 * c + 32, q0 * P:(q0 + count) * P],
                                 v_ones[:, j, h0 + c, :], prob[(first + c) % P_RING][:, at * P:(at + count) * P],
                                 start=(u < 2), stop=final, signal=pe_pv if end else None,
                                 ns=count * P * 4 / 2.4 / G + 20)
            pv_of_set.append(done)
            if final:
                pv_done[g] = done
                when(done, o_store, g)

        scaled_read = [None]
        inv_rows_read, inv_wide_read, attn_read, attn_done = [None], [None], [None], {}

        def o_store(g):
            e = g % 2
            act.wait(pv_done[g], *scaled_read)
            t = act.do(SE.copy, o_sb[:, :], o_ps[:, :], signal=act_o)
            o_read[0] = t
            o_stored[0] = g + 1
            first = HD * (1 - e)
            sp.wait(t)
            t = sp.do(DMA.dma_start, sums[:, :], o_sb[first::P // G, :], signal=s_sums)
            when(t, invert, g, t)

        def invert(g, t):
            dve.wait(t)
            t = dve.do(VE.reciprocal, sums[:, :], sums[:, :], signal=dve_dense)
            sp.wait(t, inv_rows_read[0], constants)
            t = sp.do(DMA.dma_start, inv_rows[::P // G, :], sums[:, :], signal=s_inv)
            when(t, spread, g, t)

        def spread(g, t):
            e, r = g % 2, (g % GROUPS) // 2
            mask = [1] * 32
            mask[e * HD:(e + 1) * HD] = [0] * HD
            dve.wait(t)
            scaled_halves = []
            for half in range(HALVES):
                cols = slice(half * BANK, (half + 1) * BANK)
                dve.wait(inv_wide_read[0])
                t = dve.do(VE.stream_shuffle, inv_wide[:, :], inv_rows[:, cols], mask, signal=dve_dense)
                inv_rows_read[0] = t
                scaled = attn[:, r, cols] if e == 0 else o_sb[:, cols]
                t = combine(scaled, o_sb[:, cols], inv_wide[:, :], ALU.mult, t, attn_read[0])
                inv_wide_read[0] = t
                if e == 1:
                    t = combine(attn[:, r, cols], attn[:, r, cols], scaled, ALU.add, t, *attn_done[g - 1])
                scaled_halves.append(t)
            scaled_read[:] = scaled_halves
            attn_done[g] = scaled_halves

        ln_turn, ln_open, ln_used = [0], [False] * LN_RING, [None] * LN_RING

        def layer_norm(bank, n, residual, outs, before, finish):
            k = ln_turn[0] % LN_RING
            ln_turn[0] += 1
            assert not ln_open[k]
            ln_open[k] = True
            y, stats, mv = ln_in[k], ln_stats[k], ln_mv[k]
            dve.wait(ln_used[k], *before)
            t = dve.do(VE.tensor_tensor, y[:, :, :], bank[:, :].rearrange("p (i d) -> p i d", i=2), residual,
                       ALU.add, signal=dve_dense)
            bank_was_read(n, t)
            dve.wait(t)
            for i in range(2):
                t = dve.do(VE.bn_stats, stats[:, i, :], y[:, i, :], signal=dve_dense)
            dve.wait(t)
            for i in range(2):
                t = dve.do(VE.bn_aggr, mv[:, i, :], stats[:, i, :], signal=dve_dense)
            dve.wait(t)
            t = dve.do(VE.tensor_scalar, ln_var[k][:, :], mv[:, :, 1], EPS, None, ALU.add, signal=dve_dense)
            pool.wait(t, constants)
            t = pool.do(GE.tensor_tensor, ln_rstd[k][:, :], ln_var[k][:, :], minus_half[:, :], ALU.pow,
                        signal=pool_dense)
            when(t, normalise, k, outs, t, finish)

        def normalise(k, outs, t, finish):
            dve.wait(t)
            y = ln_in[k]
            for i in range(2):
                t = dve.do(VE.tensor_scalar, outs[i] if outs else y[:, i, :], y[:, i, :], ln_mv[k][:, i, 0:1],
                           ln_rstd[k][:, i:i + 1], ALU.subtract, ALU.mult, signal=dve_dense)
            ln_used[k], ln_open[k] = t, False
            finish(t, k)

        x1 = [x1_sb] * (B - 1) + [xT_sb[:, :, :].rearrange("p m t -> p (m t)").rearrange("p (c d) -> p c d", d=D)]
        x_ready, x1_used, x1_done = {}, {}, {}

        def load_x(b):
            sp.wait(x1_used.get((b - 1, 2 * HALVES - 1)) if b < B - 1 else xT_read[0])
            t = sp.do(DMA.dma_start, x1[b][:, :, :], x[b].rearrange("(c p) d -> p c d", p=P), signal=s_x[b])
            when(t, add_bo, b, t)

        def add_bo(b, t):
            x_ready[b] = [combine(x1[b][:, i:i + 2, :], x1[b][:, i:i + 2, :],
                                  bo_sb[:, :].rearrange("p (o d) -> p o d", o=1).broadcast_to([P, 2, D]),
                                  ALU.add, t, weights) for i in range(0, C, 2)]

        def wo_unit(b, t2):
            pe.wait(weights, *[attn_done[g][t2 * 2 // CH] for g in range(b * GROUPS, (b + 1) * GROUPS)])
            n, bank = take_bank()
            for i in range(2):
                tok = (2 * t2 + i) * P
                for r in range(PAIRS):
                    done = pe.do(TE.matmul, bank[:, i * D:(i + 1) * D], attn[:, r, tok:tok + P], wo_sb[:, r, :],
                                 start=(r == 0), stop=(r == PAIRS - 1), signal=pe_dense if i and r else None)
                    if not (i and r):
                        yield
            attn_read[0] = done
            when(done, ln1, b, t2, n, bank, done)

        def ln1(b, t2, n, bank, done):
            rows = x1[b][:, 2 * t2:2 * t2 + 2, :]

            def finish(t, k):
                x1_done[(b, t2)] = t
                when(t, add_up, b, t2, t)

            layer_norm(bank, n, rows, [rows[:, 0, :], rows[:, 1, :]], [done, x_ready[b][t2]], finish)

        sum_done, sums_added, mean_done = {}, {}, {}

        def add_up(b, t2, t):
            rows = x1[b][:, 2 * t2:2 * t2 + 2, :]
            for i in range(2):
                if t2 or i:
                    before = x1_sum[:, :] if t2 else rows[:, 0, :]
                    sum_done[b] = combine(x1_sum[:, :], before, rows[:, i, :], ALU.add, t,
                                          sum_done.get(b), mean_done.get(b - 1))
            sums_added.setdefault(b, []).append(t2)

        def sum_unit(b):
            pe.wait(sum_done[b], constants)
            n, bank = take_bank()
            for m in range(M):
                done = pe.do(TE.matmul, bank[:, m:m + 1], x1_sum[:, m * P:(m + 1) * P], ones[:, :], start=True,
                             stop=True, signal=pe_dense if m == M - 1 else None, ns=430)
            when(done, store_sums, b, n, bank, done)
            yield

        def store_sums(b, n, bank, done):
            dve.wait(done)
            t = mean_done[b] = dve.do(VE.tensor_scalar, x1_mean[:, :], bank[:, 0:M], 1.0 / T, None, ALU.mult,
                                      signal=dve_dense)
            bank_was_read(n, t)

        def route_unit(b):
            pe.wait(mean_done[b], weights)
            n, bank = take_bank()
            for m in range(M):
                done = pe.do(TE.matmul, bank[0:1, 0:E], x1_mean[:, m:m + 1], wr_sb[:, m, :], start=(m == 0),
                             stop=(m == M - 1), signal=pe_dense if m == M - 1 else None, ns=100)
            when(done, pick, b, n, bank, done)
            yield

        def pick(b, n, bank, done):
            dve.wait(done, weights)
            t = dve.do(VE.tensor_tensor, route[:, :], bank[0:1, 0:E], br_sb[:, :], ALU.add, signal=dve_dense)
            bank_was_read(n, t)
            dve.wait(t)
            t = dve.do(VE.max, route_top[:, :], route[:, :], signal=dve_dense)
            dve.wait(t, bias_loaded.get(b - 1))
            t = dve.do(VE.max_index, route_at[:, :], route_top[:, :], route[:, :], signal=dve_dense)
            when(t, load_expert, b, t)

        staging = stage + prob
        staging_used, staging_turn = [()] * len(staging), [0]

        def take_staging():
            staging_turn[0] += 1
            return staging_turn[0] % STAGE_RING

        w_used, bias_loaded, w_split, b2_added = [None], {}, {}, {}
        experts = {}

        def split(k, hi, lo, *before):
            src = staging[k][:, :]
            if act.clock < dve.clock:
                act.wait(*before)
                t = act.do(SE.copy, hi, src, signal=act_dense)
            else:
                dve.wait(*before)
                t = dve.do(VE.tensor_copy, hi, src, signal=dve_dense, ns=340)
            u = combine(lo, src, hi.bitcast(F32), ALU.subtract, t, *before)
            staging_used[k] = (t, u)
            return u

        def load_expert(b, t):
            sp.wait(t, w_used[0], *[b2_added.get((b - 1, q)) for q in range(2 * HALVES)])

            def read_index():
                experts[b] = nc.sync.value_load(route_at[0:1, 0:1], min_val=0, max_val=E - 1)

            sp.do(read_index)
            for chunk in range(chunks_ahead(b)):
                load_chunk(b, chunk)
            sp.do(lambda: nc.sync.dma_start(
                b1_sb[:, :], b1T[bass.ds(experts[b], 1), :, :].rearrange("e p f -> p (e f)")), signal=s_bias)
            bias_loaded[b] = sp.do(lambda: nc.sync.dma_start(
                b2_sb[:, :], b2[bass.ds(experts[b], 1), :].broadcast_to([P, D])), signal=s_bias)
            for half in range(HALVES):
                when(bias_loaded[b], add_b2, b, half)

        def chunks_ahead(b):
            return STAGE_RING if b < B - 1 else P_RING

        def load_chunk(b, chunk):
            if b < B - 1:
                k = take_staging()
                sp.wait(*staging_used[k])
            else:
                k = STAGE_RING + chunk
                sp.wait(pv_of_set[-1])
            if chunk < CHUNKS:
                m, f0 = chunk // (F // BANK), chunk % (F // BANK) * BANK

                def issue():
                    return nc.sync.dma_start(staging[k][:, :], w1[bass.ds(experts[b], 1), m * P:(m + 1) * P,
                                                                f0:f0 + BANK].rearrange("e p f -> p (e f)"))
                hi, lo = (w[:, m, f0:f0 + BANK] for w in (w1_hi, w1_lo))
            else:
                f = (chunk - CHUNKS) * (BANK // D)

                def issue():
                    rows = w2[bass.ds(experts[b], 1), f * P:f * P + (BANK // D) * P, :]
                    return nc.sync.dma_start(staging[k][:, :].rearrange("p (f d) -> p f d", d=D),
                                             rows.rearrange("e (f p) d -> p (e f) d", p=P))
                hi, lo = (w[:, f:f + BANK // D, :].rearrange("p f d -> p (f d)") for w in (w2_hi, w2_lo))
            t = sp.do(issue, signal=s_stage[k])
            when(t, split_chunk, b, chunk, k, hi, lo, t)

        def split_chunk(b, chunk, k, hi, lo, t):
            done = split(k, hi, lo, t, w_used[0])
            w_split.setdefault(b, []).append(done)
            if chunk + chunks_ahead(b) < 2 * CHUNKS:
                load_chunk(b, chunk + chunks_ahead(b))

        def add_b2(b, half):
            if (b, half) not in x1_turned:
                b2_waits.add((b, half))
                return
            for q in (2 * half, 2 * half + 1):
                rows = x1[b][:, 2 * q:2 * q + 2, :]
                bias = b2_sb[:, :].rearrange("p (o d) -> p o d", o=1).broadcast_to([P, 2, D])
                b2_added[(b, q)] = combine(rows, rows, bias, ALU.add, bias_loaded[b], x1_turned[(b, half)], sum_done[b])

        x1T_done, x1T_used, x1_turned, b2_waits = {}, [None], {}, set()

        def turn_unit(b, half, m):
            pe.wait(x1_done[(b, 2 * half)], x1_done[(b, 2 * half + 1)], constants)
            n, bank = take_bank()
            for i in range(CH):
                done = pe.do(TE.transpose, bank[:, i * P:(i + 1) * P],
                             x1[b][:, half * CH + i, m * P:(m + 1) * P], identity[:, :],
                             signal=pe_dense if i == CH - 1 else None, ns=109)
            if m == M - 1:
                x1_turned[(b, half)] = done
                if (b, half) in b2_waits:
                    when(done, add_b2, b, half)
            when(done, turn_store, b, half, m, n, bank, done)
            yield

        def turn_store(b, half, m, n, bank, done):
            hi, lo = x1T_hi[:, m, :], x1T_lo[:, m, :]
            act.wait(done, x1T_used[0])
            t = act.do(SE.copy, hi, bank[:, :], signal=act_dense)
            dve.wait(t)
            t = dve.do(VE.tensor_tensor, lo, bank[:, :], hi.bitcast(F32), ALU.subtract, signal=dve_dense)
            bank_was_read(n, t)
            x1T_done.setdefault((b, half), []).append(t)

        hidden_done, hidden_used = {}, [None]

        def ffn1_unit(b, q, f2):
            half = q // 2
            tok = slice((q % 2) * QT, (q % 2 + 1) * QT)
            pe.wait(*w_split[b][:CHUNKS], *x1T_done[(b, half)])
            n, bank = take_bank()
            for i in range(2):
                cols = slice((2 * f2 + i) * P, (2 * f2 + i + 1) * P)
                for m in range(M):
                    for w, a in ((w1_hi, x1T_hi), (w1_hi, x1T_lo), (w1_lo, x1T_hi)):
                        first, last = w is w1_hi and a is x1T_hi, w is w1_lo
                        done = pe.do(TE.matmul, bank[:, i * QT:(i + 1) * QT], w[:, m, cols], a[:, m, tok],
                                     start=(m == 0 and first), stop=(m == M - 1 and last),
                                     signal=pe_dense if i and m == M - 1 and last else None)
                if i == 0:
                    yield
            if q % 2 and f2 == FC // 2 - 1:
                x1T_used[0] = done
                if q == 2 * HALVES - 1:
                    ffn1_over.add(b)
            when(done, relu, b, q, f2, n, bank, done)
            yield

        def relu(b, q, f2, n, bank, done):
            k = take_staging()
            act.wait(done, bias_loaded[b], *staging_used[k])
            for i in range(2):
                cols = slice(i * QT, (i + 1) * QT)
                t = act.do(SE.activation, staging[k][:, cols], bank[:, cols], ACT.Relu,
                           bias=b1_sb[:, 2 * f2 + i:2 * f2 + i + 1], scale=1.0, signal=act_dense)
            bank_was_read(n, t)
            hi, lo = (h[:, 2 * f2:2 * f2 + 2, :].rearrange("p f t -> p (f t)") for h in (hidden_hi, hidden_lo))
            done = split(k, hi, lo, t, hidden_used[0])
            hidden_done.setdefault((b, q), []).append(done)

        def ffn2_unit(b, q):
            pe.wait(*w_split[b])
            n, bank = take_bank()
            for i in range(2):
                tok = slice(i * P, (i + 1) * P)
                for f in range(FC):
                    pe.wait(hidden_done[(b, q)][f // 2])
                    for h, w in ((hidden_hi, w2_hi), (hidden_hi, w2_lo), (hidden_lo, w2_hi)):
                        first, last = w is w2_hi and h is hidden_hi, h is hidden_lo
                        end = f == FC - 1 and last
                        done = pe.do(TE.matmul, bank[:, i * D:(i + 1) * D], h[:, f, tok], w[:, f, :],
                                     start=(f == 0 and first), stop=end, signal=pe_dense if i and end else None)
                    if f % 2 and not (i and f == FC - 1):
                        yield
            hidden_used[0] = done
            if q == 2 * HALVES - 1:
                w_used[0] = done
                ffn2_over.add(b)
            when(done, ln2, b, q, n, bank, done)
            yield

        def ln2(b, q, n, bank, done):
            def finish(t, k):
                rows = out[b].rearrange("(c p) d -> p c d", p=P)
                sp.wait(t)
                ln_used[k] = sp.do(DMA.dma_start, rows[:, 2 * q:2 * q + 2, :], ln_in[k][:, :, :], signal=s_out[k])

            layer_norm(bank, n, x1[b][:, 2 * q:2 * q + 2, :], None, [done, b2_added[(b, q)]], finish)
            x1_used[(b, q)] = bank_read[n]

        def parts_ready(p):
            return len(parts_done.get(p, ())) == 2 * HALVES

        def v_turn(t2):
            return max(0, G * min(u for u in range(UNITS) if v_needed(u) >= t2) - V_LEAD)

        def v_stream():
            for b in range(B):
                for t2 in range(C // 2):
                    yield (b * GROUPS * SLOTS + v_turn(t2),
                           lambda b=b: xT_loaded[b] and (b == 0 or b * GROUPS - 1 in pv_done), v_unit(b, t2))

        def qk_stream():
            for p in range(B * PAIRS):
                for i in range(2 * HALVES):
                    yield ((2 * p - 3) * SLOTS + QK_AT + QK_EVERY * i,
                           lambda p=p: xT_loaded[p // PAIRS] and (p == 0 or len(fill_done.get(2 * p - 1, ())) == G
                                                                  and fill_done[2 * p - 1][-1][2] <= pe.clock),
                           qk_unit(p, i % 2, i // 2))

        ffn1_over, ffn2_over = {-1}, {-1}

        def post_stream(b):
            def w_ready():
                return len(w_split.get(b, ())) >= (2 if b < B - 1 else 1) * CHUNKS

            units = [(lambda: (b + 1) * GROUPS - 1 in attn_done and b in x_ready, wo_unit(b, t2), 1)
                     for t2 in range(C // 2)]
            units += [(lambda: len(sums_added.get(b, ())) == C // 2, sum_unit(b), .5),
                      (lambda: b in mean_done and b - 1 in ffn2_over, route_unit(b), .2)]

            def turns(half):
                return [(lambda: (b, 2 * half + 1) in x1_done and b - 1 in ffn1_over, turn_unit(b, half, m), .3)
                        for m in range(M)]

            units += turns(0)
            for q in range(2 * HALVES):
                units += [(lambda q=q: w_ready() and len(x1T_done.get((b, q // 2), ())) == M, ffn1_unit(b, q, f2), .8)
                          for f2 in range(FC // 2)]
                if q % 2 and q // 2 + 1 < HALVES:
                    units += turns(q // 2 + 1)
                units += [(lambda q=q: len(hidden_done.get((b, q), ())) == FC // 2 and (b, q) in b2_added and
                           len(w_split[b]) == 2 * CHUNKS, ffn2_unit(b, q), 3.1)]
            at, span = (b + 1) * GROUPS * SLOTS + POST_AT, GROUPS * SLOTS - POST_END
            if b == B - 2:
                span += TAIL
            if b == B - 1:
                at = span = 0
            total, done = sum(u[2] for u in units), 0
            for ready, unit, weight in units:
                yield (at + span * done / total, ready, unit)
                done += weight

        for i in (1, 2):
            when((None, None, OPEN_AT * i), open_rows, i)

        streams = [list(v_stream()), list(qk_stream()), *[list(post_stream(b)) for b in range(B)]]
        exps = maxes = sets = 0
        dense_unit = None
        fills, next_x, next_xT = 0, 0, 1

        def started(*tokens):
            return max([pe.clock] + [t[2] for t in tokens if t])

        while True:
            run_deferred(pe.clock)
            if fills < LAST * G and sp.clock < pe.clock + 2000:
                g, c = fills // G, fills % G
                if parts_ready(g // 2) and rows_open[g % 3] and (g < 3 or g - 3 in exp_read):
                    fill(g, c)
                    fills += 1
            if next_xT < B and not dense_unit and all(
                    len(stream) <= (B - next_xT) * units_of_row for stream, units_of_row in
                    ((streams[0], C // 2), (streams[1], PAIRS * 2 * HALVES))):
                xT_loaded[next_xT] = load_xT(next_xT)
                next_xT += 1
            if pe.clock > X_AT and (next_x < B - 1 and (next_x == 0 or (next_x - 1, 2 * HALVES - 1) in x1_used) or
                                    next_x == B - 1 and not streams[0] and not streams[1] and not dense_unit):
                load_x(next_x)
                next_x += 1

            choices = []
            if exps < LAST * SLOTS:
                g = exps // SLOTS
                if g in maxrow_done and len(exp_done) > exps - 2 and (
                        exps < P_RING or len(pv_of_set) > (exps - P_RING) // G):
                    choices.append((exps, started(maxrow_done[g], exp_done[exps - 2] if exps > 1 else None), "exp"))
            if maxes < LAST * SLOTS:
                g, n = maxes // SLOTS, maxes % SLOTS
                if len(fill_done.get(g, ())) > n // UNITS and len(max_done) > maxes - 2 and (g < 1 or g - 1 in maxrow_done):
                    choices.append(((g - 1) * SLOTS - MAX_LEAD + n * MAX_SLOTS / SLOTS,
                                    started(fill_done[g][n // UNITS], max_done[maxes - 2] if maxes > 1 else None), "max"))
            if sets < LAST * UNITS:
                g, u = sets // UNITS, sets % UNITS
                if len(prob_done) >= G * (sets + 1) and len(v_done.get(g // GROUPS, ())) > v_needed(u) and (
                        u or g == 0 or o_stored[0] == g):
                    at = started(prob_done[G * sets + G - 1], o_read[0], v_done[g // GROUPS][v_needed(u)])
                    choices.append((G * sets + PV_AT, at, "pv"))
            if dense_unit:
                choices.append((dense_unit[0], pe.clock, "go on"))
            elif bank_ready():
                free = started(bank_read[banks_taken[0] % 2])
                if turns_due:
                    choices.append((-1, max(free, turns_due[0][1][2]), "turn"))
                for i, stream in enumerate(streams):
                    if stream and stream[0][1]():
                        choices.append((stream[0][0], free, i))
            if not choices:
                if not deferred:
                    break
                pe.clock = max(pe.clock, min(deferred)[0])
                continue
            near = [c for c in choices if c[1] <= pe.clock + NEAR]
            turn, at, what = min(near, key=lambda c: c[0]) if near else min(choices, key=lambda c: c[1])
            if not near and deferred and min(deferred)[0] < at:
                pe.clock = max(pe.clock, min(deferred)[0])
                continue
            if what == "exp":
                exp_unit(exps // SLOTS, exps % SLOTS)
                exps += 1
            elif what == "max":
                max_unit(maxes // SLOTS, maxes % SLOTS)
                maxes += 1
            elif what == "pv":
                pv_set(sets // UNITS, sets % UNITS)
                sets += 1
            elif what == "turn":
                max_turn(*turns_due.pop(0))
            else:
                if what != "go on":
                    dense_unit = streams[what].pop(0)
                if next(dense_unit[2], "end") == "end":
                    dense_unit = None
        assert exps == maxes == LAST * SLOTS and sets == LAST * UNITS and not any(streams)
        sp.wait(*[(s, s.count, 0) for s in s_out])

        block = ctx.enter_context(nc.Block())

        @block.tensor
        def _(engine):
            pe.play(engine)

        @block.vector
        def _(engine):
            dve.play(engine)

        @block.scalar
        def _(engine):
            act.play(engine)

        @block.gpsimd
        def _(engine):
            pool.play(engine)

        @block.sync
        def _(engine):
            sp.play(engine)


def kernel(L0_attn_x, L0_attn_wq, L0_attn_bq, L0_attn_wk, L0_attn_bk, L0_attn_wv, L0_attn_bv, L0_attn_wo,
           L0_attn_bo, L0_ffn_Wr, L0_ffn_br, L0_ffn_W1, L0_ffn_b1, L0_ffn_W2, L0_ffn_b2):
    import numpy as np
    import concourse.bacc as bacc
    from concourse.bass_utils import run_bass_kernel_spmd

    x = np.asarray(L0_attn_x)
    D = x.shape[-1]
    E = L0_ffn_W1.shape[0]
    wo = np.asarray(L0_attn_wo).reshape(D // P, 2, G, HD, D).transpose(0, 2, 1, 3, 4).reshape(D, D)
    bqkT = np.stack([np.asarray(L0_attn_bq).reshape(-1, P).T, np.asarray(L0_attn_bk).reshape(-1, P).T], axis=1)
    layouts = {
        "x": x, "xT": x.transpose(0, 2, 1),
        "wq": L0_attn_wq, "wk": L0_attn_wk, "wv": L0_attn_wv, "bqkT": bqkT,
        "bv": np.asarray(L0_attn_bv).reshape(1, -1), "wo": wo, "bo": np.asarray(L0_attn_bo).reshape(1, -1),
        "wr": L0_ffn_Wr, "br": np.asarray(L0_ffn_br).reshape(1, -1),
        "w1": L0_ffn_W1, "b1T": np.asarray(L0_ffn_b1).reshape(E, -1, P).transpose(0, 2, 1),
        "w2": L0_ffn_W2, "b2": L0_ffn_b2,
    }
    nc = bacc.Bacc("TRN2", target_bir_lowering=False, num_devices=1)
    arrays, args = {}, []
    for name, a in layouts.items():
        a = np.ascontiguousarray(a)
        arrays[f"in_{name}"] = a
        args.append(nc.dram_tensor(f"in_{name}", a.shape, mybir.dt.from_np(a.dtype), kind="ExternalInput").ap())
    out = nc.dram_tensor("out", x.shape, mybir.dt.from_np(x.dtype), kind="ExternalOutput").ap()
    post_ln_layer(nc, *args, out)
    r = run_bass_kernel_spmd(nc, [arrays], core_ids=[0])
    return r.results[0]["out"]
```
